# Optimizing a Trainium2 kernel written in Bass

```python
import numpy as np
import jax
import jax.numpy as jnp

def _softmax(x, axis=-1):
    return jax.nn.softmax(x, axis=axis)

def _gelu(x):
    return jax.nn.gelu(x, approximate=True)

def _silu(x):
    return jax.nn.silu(x)

def _sigmoid(x):
    return jax.nn.sigmoid(x)

def _layernorm(x, axis=-1, eps=1e-05):
    m = jnp.mean(x, axis=axis, keepdims=True)
    v = jnp.var(x, axis=axis, keepdims=True)
    return (x - m) / jnp.sqrt(v + eps)

def _scatter_add(tgt, idx, src, axis=0):
    return tgt.at[idx].add(src)

def _segment_sum(src, seg, n):
    return jax.ops.segment_sum(src, seg, n)
kernel_name = 'mk_vit_tower_d1_tok_img1024_r4_e6463e'

def setup_inputs(seed: int=0):
    np.random.seed(seed)
    _w = jnp.asarray

    def _rec_inputs():
        import jax
        import jax.numpy as jnp
        _rk = jax.random.key(seed)
        x = -0.000392918 + 0.999932 * jax.random.normal(jax.random.fold_in(_rk, 1), (16, 256, 256, 1), jnp.float32)
        return x
    x = _rec_inputs()

    def _L0_tok_setup():
        import jax, jax.numpy as jnp
        import numpy as np
        INV_SQRT2 = 0.7071067811865476
        LEVEL = 3

        def _split(x, axis):
            ax = axis % x.ndim
            sl0 = [slice(None)] * x.ndim
            sl0[ax] = slice(0, None, 2)
            sl1 = [slice(None)] * x.ndim
            sl1[ax] = slice(1, None, 2)
            x0, x1 = (x[tuple(sl0)], x[tuple(sl1)])
            return ((x0 + x1) * INV_SQRT2, (x0 - x1) * INV_SQRT2)

        def _merge(lo, hi, axis):
            ax = axis % lo.ndim
            e = (lo + hi) * INV_SQRT2
            o = (lo - hi) * INV_SQRT2
            s = jnp.stack([e, o], axis=ax + 1)
            shape = list(lo.shape)
            shape[ax] *= 2
            return s.reshape(shape)

        def _dwt2(x):
            lo, hi = _split(x, -1)
            a, h = _split(lo, -2)
            v, d = _split(hi, -2)
            return (a, h, v, d)

        def _idwt2(a, h, v, d):
            lo = _merge(a, h, -2)
            hi = _merge(v, d, -2)
            return _merge(lo, hi, -1)
        key = jax.random.key(seed)
        ks = jax.random.split(key, 8)
        B, H, W = (16, 256, 256)
        x = jax.random.normal(ks[0], (B, H, W, 1), dtype=jnp.float32)
        na = H // 8 * (W // 8)
        n2 = H // 4 * (W // 4)
        n1 = H // 2 * (W // 2)
        scale = 0.02
        Wa = jax.random.normal(ks[1], (na, 1), dtype=jnp.float32) * scale
        ba = jnp.zeros((1,), jnp.float32)
        Wd1 = jax.random.normal(ks[2], (3 * na, 3), dtype=jnp.float32) * scale
        bd1 = jnp.zeros((3,), jnp.float32)
        Wd2 = jax.random.normal(ks[3], (3 * n2, 3), dtype=jnp.float32) * scale
        bd2 = jnp.zeros((3,), jnp.float32)
        Wd3 = jax.random.normal(ks[4], (3 * n1, 3), dtype=jnp.float32) * scale
        bd3 = jnp.zeros((3,), jnp.float32)
        return {'x': x, 'Wa': Wa, 'ba': ba, 'Wd1': Wd1, 'bd1': bd1, 'Wd2': Wd2, 'bd2': bd2, 'Wd3': Wd3, 'bd3': bd3}
    _L0_tok_all = _L0_tok_setup()
    _L0_tok_in = {k: v for k, v in _L0_tok_all.items() if k in ('Wa', 'ba', 'Wd1', 'bd1', 'Wd2', 'bd2', 'Wd3', 'bd3')}
    del _L0_tok_all

    def _L0_attn_setup():
        import jax, jax.numpy as jnp
        import numpy as np
        D_MODEL = 256
        NUM_HEADS = 16
        D_H = D_MODEL // NUM_HEADS
        BATCH, SEQ = (4, 512)
        key = jax.random.key(seed)
        kx, kq, kk, kv, ko = jax.random.split(key, 5)
        sigma = (2.0 / (D_MODEL + D_MODEL)) ** 0.5

        def trunc(k):
            return jax.random.truncated_normal(k, -3.0, 3.0, (D_MODEL, D_MODEL), dtype=jnp.float32) * sigma
        return {'x': jax.random.normal(kx, (BATCH, SEQ, D_MODEL), dtype=jnp.float32), 'Wq': trunc(kq), 'Wk': trunc(kk), 'Wv': trunc(kv), 'Wo': trunc(ko)}
    _L0_attn_all = _L0_attn_setup()
    _L0_attn_in = {k: v for k, v in _L0_attn_all.items() if k in ('Wq', 'Wk', 'Wv', 'Wo')}
    del _L0_attn_all

    def _L0_ffn_setup():
        import jax, jax.numpy as jnp
        import numpy as np
        from jax import lax
        T, B, I, M, O = (64, 64, 256, 256, 256)

        def _xavier(key, shape):
            fan_out, fan_in = shape
            limit = float(np.sqrt(6.0 / (fan_in + fan_out)))
            return jax.random.uniform(key, shape, jnp.float32, -limit, limit)
        key = jax.random.key(seed)
        ks = jax.random.split(key, 9)
        x = jax.random.normal(ks[0], (T, B, I), jnp.float32)
        return {'x': x, 'wf': _xavier(ks[1], (M, I)), 'uf': _xavier(ks[2], (M, M)), 'bf': jnp.zeros((M,), jnp.float32), 'wi': _xavier(ks[3], (M, I)), 'ui': _xavier(ks[4], (M, M)), 'bi': jnp.zeros((M,), jnp.float32), 'wc': _xavier(ks[5], (M, I)), 'uc': _xavier(ks[6], (M, M)), 'bc': jnp.zeros((M,), jnp.float32), 'wo': _xavier(ks[7], (O, I)), 'uo': _xavier(ks[8], (O, M)), 'bo': jnp.zeros((O,), jnp.float32), 'in_c': jnp.zeros((M,), jnp.float32)}
    _L0_ffn_all = _L0_ffn_setup()
    _L0_ffn_in = {k: v for k, v in _L0_ffn_all.items() if k in ('wf', 'uf', 'bf', 'wi', 'ui', 'bi', 'wc', 'uc', 'bc', 'wo', 'uo', 'bo', 'in_c')}
    del _L0_ffn_all
    return {'x': x, 'L0_tok_Wa': _L0_tok_in['Wa'], 'L0_tok_ba': _L0_tok_in['ba'], 'L0_tok_Wd1': _L0_tok_in['Wd1'], 'L0_tok_bd1': _L0_tok_in['bd1'], 'L0_tok_Wd2': _L0_tok_in['Wd2'], 'L0_tok_bd2': _L0_tok_in['bd2'], 'L0_tok_Wd3': _L0_tok_in['Wd3'], 'L0_tok_bd3': _L0_tok_in['bd3'], 'L0_attn_Wq': _L0_attn_in['Wq'], 'L0_attn_Wk': _L0_attn_in['Wk'], 'L0_attn_Wv': _L0_attn_in['Wv'], 'L0_attn_Wo': _L0_attn_in['Wo'], 'L0_ffn_wf': _L0_ffn_in['wf'], 'L0_ffn_uf': _L0_ffn_in['uf'], 'L0_ffn_bf': _L0_ffn_in['bf'], 'L0_ffn_wi': _L0_ffn_in['wi'], 'L0_ffn_ui': _L0_ffn_in['ui'], 'L0_ffn_bi': _L0_ffn_in['bi'], 'L0_ffn_wc': _L0_ffn_in['wc'], 'L0_ffn_uc': _L0_ffn_in['uc'], 'L0_ffn_bc': _L0_ffn_in['bc'], 'L0_ffn_wo': _L0_ffn_in['wo'], 'L0_ffn_uo': _L0_ffn_in['uo'], 'L0_ffn_bo': _L0_ffn_in['bo'], 'L0_ffn_in_c': _L0_ffn_in['in_c']}

def reference(x, L0_tok_Wa, L0_tok_ba, L0_tok_Wd1, L0_tok_bd1, L0_tok_Wd2, L0_tok_bd2, L0_tok_Wd3, L0_tok_bd3, L0_attn_Wq, L0_attn_Wk, L0_attn_Wv, L0_attn_Wo, L0_ffn_wf, L0_ffn_uf, L0_ffn_bf, L0_ffn_wi, L0_ffn_ui, L0_ffn_bi, L0_ffn_wc, L0_ffn_uc, L0_ffn_bc, L0_ffn_wo, L0_ffn_uo, L0_ffn_bo, L0_ffn_in_c):
    import jax
    import jax.numpy as jnp

    def _L0_tok_ref(x, Wa, ba, Wd1, bd1, Wd2, bd2, Wd3, bd3):
        import jax, jax.numpy as jnp
        import numpy as np
        INV_SQRT2 = 0.7071067811865476
        LEVEL = 3

        def _split(x, axis):
            ax = axis % x.ndim
            sl0 = [slice(None)] * x.ndim
            sl0[ax] = slice(0, None, 2)
            sl1 = [slice(None)] * x.ndim
            sl1[ax] = slice(1, None, 2)
            x0, x1 = (x[tuple(sl0)], x[tuple(sl1)])
            return ((x0 + x1) * INV_SQRT2, (x0 - x1) * INV_SQRT2)

        def _merge(lo, hi, axis):
            ax = axis % lo.ndim
            e = (lo + hi) * INV_SQRT2
            o = (lo - hi) * INV_SQRT2
            s = jnp.stack([e, o], axis=ax + 1)
            shape = list(lo.shape)
            shape[ax] *= 2
            return s.reshape(shape)

        def _dwt2(x):
            lo, hi = _split(x, -1)
            a, h = _split(lo, -2)
            v, d = _split(hi, -2)
            return (a, h, v, d)

        def _idwt2(a, h, v, d):
            lo = _merge(a, h, -2)
            hi = _merge(v, d, -2)
            return _merge(lo, hi, -1)
        img = x[..., 0]
        B = img.shape[0]
        details = []
        cur = img
        for _ in range(LEVEL):
            cur, h, v, d = _dwt2(cur)
            details.append((h, v, d))
        aw = jax.nn.sigmoid(cur.reshape(B, -1) @ Wa + ba)
        rec = cur * aw[:, :, None]
        det_params = [(Wd1, bd1), (Wd2, bd2), (Wd3, bd3)]
        for (h, v, d), (Wd, bd) in zip(reversed(details), det_params):
            flat = jnp.stack([h, v, d], axis=1).reshape(B, -1)
            w = jax.nn.softmax(flat @ Wd + bd, axis=-1)
            rec = _idwt2(rec, h * w[:, 0, None, None], v * w[:, 1, None, None], d * w[:, 2, None, None])
        return rec

    def _L0_attn_ref(x, Wq, Wk, Wv, Wo):
        import jax, jax.numpy as jnp
        import numpy as np
        D_MODEL = 256
        NUM_HEADS = 16
        D_H = D_MODEL // NUM_HEADS
        BATCH, SEQ = (4, 512)
        B, S, D = x.shape
        H, Dh = (NUM_HEADS, D_H)
        q = jnp.einsum('oi,bsi->bso', Wq, x)
        k = jnp.einsum('oi,bsi->bso', Wk, x)
        v = jnp.einsum('oi,bsi->bso', Wv, x)
        q = q.reshape(B, S, H, Dh).transpose(0, 2, 1, 3)
        k = k.reshape(B, S, H, Dh).transpose(0, 2, 1, 3)
        v = v.reshape(B, S, H, Dh).transpose(0, 2, 1, 3)
        scale = 1.0 / jnp.sqrt(jnp.asarray(Dh, dtype=x.dtype))
        score = jnp.einsum('bhnd,bhmd->bhnm', q, k) * scale
        causal = jnp.tril(jnp.ones((S, S), dtype=bool))
        score = jnp.where(causal, score, -jnp.inf)
        attn = jax.nn.softmax(score, axis=-1)
        out = jnp.einsum('bhnm,bhmd->bhnd', attn, v)
        out = out.transpose(0, 2, 1, 3).reshape(B, S, D)
        return jnp.einsum('oi,bsi->bso', Wo, out)

    def _L0_ffn_ref(x, wf, uf, bf, wi, ui, bi, wc, uc, bc, wo, uo, bo, in_c):
        import jax, jax.numpy as jnp
        import numpy as np
        from jax import lax
        T, B, I, M, O = (64, 64, 256, 256, 256)

        def _xavier(key, shape):
            fan_out, fan_in = shape
            limit = float(np.sqrt(6.0 / (fan_in + fan_out)))
            return jax.random.uniform(key, shape, jnp.float32, -limit, limit)
        batch = x.shape[1]
        c0 = jnp.broadcast_to(in_c, (batch, in_c.shape[0]))

        def step(c, xt):
            ft = jax.nn.sigmoid(xt @ wf.T + c @ uf.T + bf)
            it = jax.nn.sigmoid(xt @ wi.T + c @ ui.T + bi)
            gt = jnp.tanh(xt @ wc.T + c @ uc.T + bc)
            c = ft * c + it * gt
            return (c, None)
        c_final, _ = lax.scan(step, c0, x)
        h = jnp.tanh(jnp.einsum('tbi,oi->tbo', x, wo) + c_final @ uo.T + bo)
        return h
    h = _L0_tok_ref(x, L0_tok_Wa, L0_tok_ba, L0_tok_Wd1, L0_tok_bd1, L0_tok_Wd2, L0_tok_bd2, L0_tok_Wd3, L0_tok_bd3)
    h = h + _L0_attn_ref(_layernorm(h, axis=-1), L0_attn_Wq, L0_attn_Wk, L0_attn_Wv, L0_attn_Wo)
    h = h + _L0_ffn_ref(_layernorm(h, axis=-1), L0_ffn_wf, L0_ffn_uf, L0_ffn_bf, L0_ffn_wi, L0_ffn_ui, L0_ffn_bi, L0_ffn_wc, L0_ffn_uc, L0_ffn_bc, L0_ffn_wo, L0_ffn_uo, L0_ffn_bo, L0_ffn_in_c)
    return h

_drawn_inputs = setup_inputs


def setup_inputs(seed=0):
    import zlib

    import numpy as np

    out = dict(_drawn_inputs(seed))
    spreads = {'L0_tok_bd1': (0.0, 0.467),
     'L0_tok_bd2': (0.0, 0.676),
     'L0_tok_bd3': (0.0, 0.8),
     'L0_ffn_bf': (0.0, 0.527),
     'L0_ffn_bi': (0.0, 0.503),
     'L0_ffn_bc': (0.0, 0.1),
     'L0_ffn_bo': (0.0, 0.1),
     'L0_ffn_in_c': (0.0, 0.8)}
    factors = {}
    for name, (base, spread) in spreads.items():
        noise = np.random.default_rng([zlib.crc32(name.encode()), seed]).standard_normal(out[name].shape)
        drawn = base * np.exp(spread * noise) if base else spread * noise
        out[name] = jnp.asarray(drawn.astype(out[name].dtype))
    for name, factor in factors.items():
        out[name] = (out[name] * factor).astype(out[name].dtype)
    return out
```

```python
from contextlib import ExitStack

import numpy as np

import concourse.bass as bass
from concourse import mybir

F32 = mybir.dt.float32
BF16 = mybir.dt.bfloat16
ALU = mybir.AluOpType
ACT = mybir.ActivationFunctionType
AX_X = mybir.AxisListType.X

P = 128
IMAGES = 16
S = 256
D = 256
HEADS = 16
DH = D // HEADS
TILES = S // P
KT = D // P
IMG = TILES * D
EPS = 1e-5
SCALE = DH ** -0.5
MASKED = -1e30

Q_BLOCKS = (0, 0, 1, 1, 0, 2)
K_BLOCKS = (0, 1, 0, 1, 2, 0)
QK_ROWS = len(Q_BLOCKS) * DH
MAX_PARTS = 2
S2_ROWS = QK_ROWS + MAX_PARTS

PAIRS = IMAGES // 2
BR, BC = 8, 128
XW = BR * BC
LEVELS = 3
BAND = [XW >> (2 * lv) for lv in range(1, LEVELS + 1)]
TOK_FWD, TOK_SCALE, TOK_INV = 12, 4, 12
TOK_STEPS = TOK_FWD + TOK_SCALE + TOK_INV
GROUPS = 4
LOGITS = 3 * GROUPS
W_OFF = {1: 0, 2: 9 * BAND[0], 3: 9 * (BAND[0] + BAND[1])}
W_A = 9 * sum(BAND)
W_ALL = W_A + BAND[2]

WQ, WK, WV, WO, WF, WI, WC, WX, UF, UI, UC, UX = range(12)

S1_BANKS = 12
S2_BANKS = 12
PROB_RING = 6
PV_GROUPS = 4

JOBS = ["WO", "XT1", "Q", "K", "V", "SUM", "XT2", "F", "I", "G", "X", "MT"]
JOB_BANK = {"WO": 0, "XT1": 1, "Q": 0, "K": 1, "V": 0, "SUM": 1, "XT2": 0, "F": 1, "I": 0, "G": 1, "X": 0, "MT": 1}
FRONT, BACK = ("XT1", "Q", "K", "V", "MT"), ("WO", "XT2", "F", "I", "G", "X")
S1_AT = {6: (0, 1), 7: (2, 3), 8: (4, 5), 9: (6, 7, 8), 10: (9, 10, 11)}
S2_AT = {2: (0, 1), 3: (2, 3), 4: (4, 5), 5: (6, 7), 6: (8, 9), 7: (10, 11)}
PV_AT = {4: 0, 5: 1, 7: 2, 8: 3}

FIRST_LOOPED, LOOPS = 2, 6
SLOTS = IMAGES + 2


def runs(t, job):
    if job == "SUM":
        return t % 2 == 0 and t // 2 + 1 < PAIRS
    return t < IMAGES if job in FRONT else 2 <= t < SLOTS


def jobs_before(t, job):
    bank = JOB_BANK[job]
    n = 1 if bank == JOB_BANK["SUM"] else 0
    for u in range(t + 1):
        for j in JOBS:
            if u == t and j == job:
                return n
            n += JOB_BANK[j] == bank and runs(u, j)


class Slot:

    def __init__(self, t, k=None):
        self.t, self.k = t, k
        self.par = t % 2
        looped = k is not None
        self.front = looped or t < IMAGES
        self.middle = looped or 1 <= t <= IMAGES
        self.back = looped or t >= 2
        self.pair = looped or t // 2 + 1 < PAIRS
        self.next_front = looped or t + 1 < IMAGES

    def has(self, job):
        if job == "SUM":
            return self.pair and self.par == 0
        return self.front if job in FRONT else self.back

    def at(self, count):
        if self.k is None:
            return count(self.t)
        return self.k * (count(self.t + 2) - count(self.t)) + count(self.t)


def wait(eng, sem, slot, count):
    if slot.k is None and count(slot.t) <= 0:
        return
    assert count(slot.t) > 0
    eng.wait_ge(sem, slot.at(count))


def all_slots(eng, body):
    for t in range(FIRST_LOOPED):
        body(Slot(t))
    with eng.Fori(0, LOOPS) as k:
        for s in range(2):
            body(Slot(FIRST_LOOPED + s, k))
    for t in range(FIRST_LOOPED + 2 * LOOPS, SLOTS):
        body(Slot(t))


def build(nc, x, weights, tok_w, tok_b, col_b, bo, out, scratch):
    ctx = ExitStack()
    with ctx:
        def sb(name, shape, dt=F32):
            return ctx.enter_context(nc.sbuf_tensor(name, shape, dt))

        def ps(name, shape):
            return ctx.enter_context(nc.psum_tensor(name, shape, F32))

        def sem(name):
            return ctx.enter_context(nc.semaphore(name))

        hidden = sb("hidden", [P, IMAGES * IMG])
        xo = sb("xo", [P, IMAGES * IMG])
        w_all = sb("w_all", [P, 12, KT, D])
        q_stack = sb("q_stack", [P, 2, HEADS, S], BF16)
        k_stack = sb("k_stack", [P, 2, HEADS, S], BF16)
        q_parts = sb("q_parts", [P, 3, 2, S], BF16)
        k_parts = sb("k_parts", [P, 3, 2, S], BF16)
        q_rest = sb("q_rest", [P, 2 * S])
        k_rest = sb("k_rest", [P, 2 * S])
        v_pad = sb("v_pad", [P, 2, TILES, HEADS // 2, 4, DH])
        ones_pad = sb("ones_pad", [P, 2, 2 * DH])
        xn1 = sb("xn1", [P, TILES, D])
        xn2 = sb("xn2", [P, TILES, D])
        xt1 = sb("xt1", [P, KT, S])
        xt2 = sb("xt2", [P, KT, S])
        probs = sb("probs", [P, PROB_RING, 512])
        row_inv = sb("row_inv", [P, 2, S])
        attn_t = sb("attn_t", [P, 2, S])
        gate = sb("gate", [P, 3, 2, S])
        c2 = sb("c2", [P, KT, S])
        neg_max = sb("neg_max", [P, TILES, HEADS])
        neg_max_parts = sb("neg_max_parts", [P, TILES, MAX_PARTS, HEADS], BF16)
        max_rows = sb("max_rows", [MAX_PARTS * HEADS, S], BF16)
        bn1 = sb("bn1", [P, TILES, 6])
        bn2 = sb("bn2", [P, TILES, 6])
        mv1 = sb("mv1", [P, TILES, 2])
        mv2 = sb("mv2", [P, TILES, 2])
        ln1 = sb("ln1", [P, 3, TILES])
        ln2 = sb("ln2", [P, 3, TILES])
        tok_x = sb("tok_x", [P, XW])
        tok_t = sb("tok_t", [P, XW])
        tok_c = {lv: sb(f"tok_c{lv}", [P, 4 * BAND[lv - 1]]) for lv in (1, 2, 3)}
        tok_weights = sb("tok_weights", [P, W_ALL])
        dots = sb("dots", [P, LOGITS])
        logit = sb("logit", [P, LOGITS])
        logit_b = sb("logit_b", [P, LOGITS])
        logit_s = sb("logit_s", [P, LOGITS])
        band_s = sb("band_s", [P, LOGITS])
        tok_max = sb("tok_max", [P, GROUPS])
        tok_sum = sb("tok_sum", [P, GROUPS])
        tok_exp = sb("tok_exp", [P, LOGITS])
        band_w = sb("band_w", [P, LOGITS])
        half_col = sb("half_col", [P, 4, KT])
        gate_b = sb("gate_b", [P, 3, KT])
        bo_row = sb("bo_row", [P, D])
        cu = sb("cu", [P, TILES, D])
        ident = sb("ident", [P, P])
        ident_b = sb("ident_b", [P, P], BF16)
        mask_qk = sb("mask_qk", [P, P], BF16)
        mask_kq = sb("mask_kq", [P, P], BF16)
        same_image = sb("same_image", [P, P])
        neg_half = sb("neg_half", [P, TILES])
        eps = sb("eps", [P, TILES])
        spare = sb("spare", [P, 1])

        stage = ps("stage", [P, 2, 512])
        s1 = ps("s1", [P, 2, 512])
        s2 = ps("s2", [P, 2, 512])
        pv = ps("pv", [P, 2, 2, S])

        consts_set = sem("consts_set")
        pool_set = sem("pool_set")
        pads_set = sem("pads_set")
        dve_set = sem("dve_set")
        tok_in = sem("tok_in")
        tokw_in = sem("tokw_in")
        small_in = sem("small_in")
        qkv_in = sem("qkv_in")
        rest_in = sem("rest_in")
        x_in = tok_in
        u_scaled = sem("u_scaled")
        tok_step = sem("tok_step")
        dots_done = sem("dots_done")
        tok_small = sem("tok_small")
        tok_exp_done = sem("tok_exp_done")
        rec_out = sem("rec_out")
        hidden_in = sem("hidden_in")
        stage_full = [sem("stage_full0"), sem("stage_full1")]
        stage_emptied = [sem("stage_emptied0"), sem("stage_emptied1")]
        q1_ready, q2_ready, q3_ready = sem("q1_ready"), sem("q2_ready"), sem("q3_ready")
        k1_ready, k2_ready, k3_ready = sem("k1_ready"), sem("k2_ready"), sem("k3_ready")
        q_stacked = sem("q_stacked")
        k_stacked = sem("k_stacked")
        max_stacked = sem("max_stacked")
        s1_full, s1_emptied = sem("s1_full"), sem("s1_emptied")
        s2_full, probs_ready = sem("s2_full"), sem("probs_ready")
        max_part1, max_parts_ready = sem("max_part1"), sem("max_parts_ready")
        pv_done, inv_ready, attn_ready = sem("pv_done"), sem("inv_ready"), sem("attn_ready")
        bn_done = [sem("bn1_done"), sem("bn2_done")]
        mv_done = [sem("mv1_done"), sem("mv2_done")]
        eps_done = [sem("eps1_done"), sem("eps2_done")]
        rstd_done = [sem("rstd1_done"), sem("rstd2_done")]
        shift_done = [sem("shift1_done"), sem("shift2_done")]
        xn_ready = [sem("xn1_ready"), sem("xn2_ready")]
        c_half = sem("c_half")
        c_ready = sem("c_ready")
        cu_ready = sem("cu_ready")
        pre_ready, tanh_ready = sem("pre_ready"), sem("tanh_ready")
        out_even, out_odd = sem("out_even"), sem("out_odd")
        stored = sem("stored")

        block = ctx.enter_context(nc.Block())

        def full(eng, slot, job):
            wait(eng, stage_full[JOB_BANK[job]], slot, lambda t: jobs_before(t, job) + 1)

        def emptied(eng, slot, job):
            wait(eng, stage_emptied[JOB_BANK[job]], slot, lambda t: jobs_before(t, job) + 1)

        def bank(job):
            return stage[:, JOB_BANK[job], :]

        def image(buf, slot, back):
            return buf[:, bass.ds(slot.at(lambda t: (t - back) * IMG), IMG)] if slot.k is not None else \
                buf[:, (slot.t - back) * IMG:(slot.t - back + 1) * IMG]

        def tok_wait(eng, slot, n):
            wait(eng, tok_step, slot, lambda t: TOK_STEPS * (t // 2 + 1) + n)

        def tok_forward(eng, slot):
            src, n = tok_x, XW
            for lv in range(1, LEVELS + 1):
                h = n // 2
                base = 4 * (lv - 1)
                even = src[:, 0:n].rearrange("p (n two) -> p two n", two=2)
                if lv > 1:
                    tok_wait(eng, slot, base)
                eng.tensor_tensor(tok_t[:, 0:h], even[:, 0], even[:, 1], ALU.add).then_inc(tok_step, 1)
                eng.tensor_tensor(tok_t[:, h:n], even[:, 0], even[:, 1], ALU.subtract).then_inc(tok_step, 1)
                c = BC >> lv
                rows = tok_t[:, 0:n].rearrange("p (m two c) -> p two m c", two=2, c=c)
                dst = tok_c[lv]
                tok_wait(eng, slot, base + 2)
                eng.tensor_tensor(dst[:, 0:h].rearrange("p (m c) -> p m c", c=c), rows[:, 0], rows[:, 1],
                                  ALU.add).then_inc(tok_step, 1)
                eng.tensor_tensor(dst[:, h:n].rearrange("p (m c) -> p m c", c=c), rows[:, 0], rows[:, 1],
                                  ALU.subtract).then_inc(tok_step, 1)
                src, n = dst, n // 4

        def tok_backward(eng, slot):
            n3 = BAND[2]
            eng.tensor_tensor(tok_c[3][:, 0:n3], tok_c[3][:, 0:n3], band_w[:, 0:1].to_broadcast([P, n3]),
                              ALU.mult).then_inc(tok_step, 1)
            for lv in (3, 2, 1):
                n, g = BAND[lv - 1], GROUPS - lv
                bands = tok_c[lv][:, n:4 * n].rearrange("p (b n) -> p b n", b=3)
                wts = band_w[:, 3 * g:3 * g + 3].unsqueeze(2).to_broadcast([P, 3, n])
                eng.tensor_tensor(bands, bands, wts, ALU.mult).then_inc(tok_step, 1)
            done = TOK_FWD + TOK_SCALE
            for lv in (3, 2, 1):
                n = 4 * BAND[lv - 1]
                h, c = n // 2, BC >> lv
                rows = tok_t[:, 0:n].rearrange("p (m two c) -> p two m c", two=2, c=c)
                src = tok_c[lv]
                av = src[:, 0:h].rearrange("p (m c) -> p m c", c=c)
                hd = src[:, h:n].rearrange("p (m c) -> p m c", c=c)
                tok_wait(eng, slot, done)
                eng.tensor_tensor(rows[:, 0], av, hd, ALU.add).then_inc(tok_step, 1)
                eng.tensor_tensor(rows[:, 1], av, hd, ALU.subtract).then_inc(tok_step, 1)
                dst = tok_x if lv == 1 else tok_c[lv - 1]
                cols = dst[:, 0:n].rearrange("p (n two) -> p two n", two=2)
                tok_wait(eng, slot, done + 2)
                eng.tensor_tensor(cols[:, 0], tok_t[:, 0:h], tok_t[:, h:n], ALU.add).then_inc(tok_step, 1)
                eng.tensor_tensor(cols[:, 1], tok_t[:, 0:h], tok_t[:, h:n], ALU.subtract).then_inc(tok_step, 1)
                done += 4

        DOTS = 10
        FIRST_PAIR = Slot(-2)

        def tok_dots(eng, slot):
            tok_wait(eng, slot, TOK_FWD)
            columns = [(0, 3, 0, BAND[2], W_A)]
            for lv in (3, 2, 1):
                n, g = 3 * BAND[lv - 1], GROUPS - lv
                columns += [(3 * g + j, lv, n // 3, n, W_OFF[lv] + j * n) for j in range(3)]
            for i, (col, lv, first, n, off) in enumerate(columns):
                products = (tok_t, tok_x)[i % 2]
                if i >= 2:
                    wait(eng, dots_done, slot, lambda t: DOTS * (t // 2 + 1) + i - 1)
                eng.tensor_tensor_reduce(products[:, 0:n], tok_c[lv][:, first:first + n], tok_weights[:, off:off + n],
                                         1.0, 0.0, ALU.mult, ALU.add, dots[:, col:col + 1]).then_inc(dots_done, 1)

        SMALL = 7

        def small_wait(eng, slot, n):
            wait(eng, tok_small, slot, lambda t: SMALL * (t // 2 + 1) + n)

        def tok_logits(eng, slot):
            l3 = logit[:, :].rearrange("p (g j) -> p g j", j=3)
            if slot is FIRST_PAIR:
                eng.wait_ge(stage_full[JOB_BANK["SUM"]], 1)
            else:
                full(eng, slot, "SUM")
            eng.tensor_tensor(logit[:, :], bank("SUM")[:, 0:LOGITS], logit_s[:, :], ALU.mult)\
               .then_inc(stage_emptied[JOB_BANK["SUM"]], 1)
            if slot is FIRST_PAIR:
                eng.wait_ge(stage_emptied[JOB_BANK["SUM"]], 1)
            else:
                emptied(eng, slot, "SUM")
            eng.tensor_tensor(logit[:, :], logit[:, :], logit_b[:, :], ALU.add).then_inc(tok_small, 1)
            small_wait(eng, slot, 1)
            eng.tensor_reduce(tok_max[:, :], l3, AX_X, ALU.max).then_inc(tok_small, 1)
            small_wait(eng, slot, 2)
            eng.tensor_tensor(l3, l3, tok_max[:, :].unsqueeze(2).to_broadcast([P, GROUPS, 3]), ALU.subtract)\
               .then_inc(tok_small, 1)

        def tok_exps(eng, slot):
            small_wait(eng, slot, 3)
            eng.activation(tok_exp[:, :], logit[:, :], ACT.Exp).then_inc(tok_exp_done, 1)

        def tok_softmax(eng, slot):
            e3 = tok_exp[:, :].rearrange("p (g j) -> p g j", j=3)
            wait(eng, tok_exp_done, slot, lambda t: t // 2 + 2)
            eng.tensor_reduce(tok_sum[:, :], e3, AX_X, ALU.add).then_inc(tok_small, 1)
            small_wait(eng, slot, 4)
            eng.reciprocal(tok_max[:, :], tok_sum[:, :]).then_inc(tok_small, 1)
            small_wait(eng, slot, 5)
            eng.tensor_tensor(e3, e3, tok_max[:, :].unsqueeze(2).to_broadcast([P, GROUPS, 3]), ALU.mult)\
               .then_inc(tok_small, 1)
            small_wait(eng, slot, 6)
            eng.tensor_tensor(band_w[:, :], tok_exp[:, :], band_s[:, :], ALU.mult).then_inc(tok_small, 1)

        def tok_sum_matmul(eng):
            eng.matmul(bank("SUM")[:, 0:LOGITS], same_image[:, :], dots[:, :], start=True, stop=True)\
               .then_inc(stage_full[JOB_BANK["SUM"]], 1)

        LN = [(bn1, mv1, ln1, xn1), (bn2, mv2, ln2, xn2)]
        LN_COUNT = [lambda t: t + 2, lambda t: t - 1]

        def ln_stats(eng, slot, which):
            bn, mv, _, _ = LN[which]
            src = image(hidden, slot, -1 if which == 0 else 2).rearrange("p (i c) -> p i c", i=TILES)
            eng.memset(spare[:, :], 0.0)
            for i in range(TILES):
                last = eng.bn_stats(bn[:, i, :], src[:, i, :])
            last.then_inc(bn_done[which], 1)
            wait(eng, bn_done[which], slot, LN_COUNT[which])
            eng.memset(spare[:, :], 0.0)
            for i in range(TILES):
                last = eng.bn_aggr(mv[:, i, :], bn[:, i, :])
            last.then_inc(mv_done[which], 1)

        def ln_rstd(eng, slot, which):
            _, mv, ln, _ = LN[which]
            wait(eng, mv_done[which], slot, LN_COUNT[which])
            eng.tensor_tensor(ln[:, 0, :], mv[:, :, 1], eps[:, :], ALU.add).then_inc(eps_done[which], 1)
            wait(eng, eps_done[which], slot, LN_COUNT[which])
            eng.tensor_tensor(ln[:, 1, :], ln[:, 0, :], neg_half[:, :], ALU.pow).then_inc(rstd_done[which], 1)

        def ln_shift(eng, slot, which):
            _, mv, ln, _ = LN[which]
            wait(eng, rstd_done[which], slot, LN_COUNT[which])
            eng.scalar_tensor_tensor(out=ln[:, 2, :], in0=mv[:, :, 0], scalar=-1.0, in1=ln[:, 1, :],
                                     op0=ALU.mult, op1=ALU.mult).then_inc(shift_done[which], 1)

        def ln_apply(eng, slot, which):
            _, _, ln, xn = LN[which]
            src = image(hidden, slot, -1 if which == 0 else 2).rearrange("p (i c) -> p i c", i=TILES)
            wait(eng, shift_done[which], slot, LN_COUNT[which])
            for i in range(TILES):
                last = eng.activation(xn[:, i, :], src[:, i, :], ACT.Identity, scale=ln[:, 1, i:i + 1],
                                      bias=ln[:, 2, i:i + 1])
            last.then_inc(xn_ready[which], 1)

        BEFORE_FIRST = Slot(-1)

        def store_pair(sp, p_value):
            sp.dma_start(scratch[bass.ds(p_value, 1)].rearrange("o p x -> (o p) x"), tok_x[:, :]).then_inc(rec_out, 16)

        def load_hidden(sp, p_value, first_image):
            pair = scratch[bass.ds(p_value, 1)].rearrange("o (i b ch) (r c) -> (o i) b r ch c", i=2, ch=2, c=BC)
            for i in range(2):
                for tile in range(TILES):
                    blocks = P // BR
                    off = (first_image + i) * IMG + tile * D
                    for ch in range(2):
                        sp.dma_start(hidden[:, bass.ds(off + ch * BC, BC)],
                                     pair[i, tile * blocks:(tile + 1) * blocks, :, ch, :]).then_inc(hidden_in, 16)

        HIDDEN_DMAS = 2 * TILES * 2 * 16

        @block.sync
        def _(sp):
            sp.dma_start(tok_x[:, :], x[0]).then_inc(tok_in, 16)
            sp.dma_start(tok_weights[:, :], tok_w).then_inc(tokw_in, 16)
            sp.dma_start(logit_b[:, 0:1], tok_b[0:1].partition_broadcast(P)).then_inc(small_in, 16)
            sp.dma_start(logit_b[:, 3:LOGITS], tok_b[1:10].partition_broadcast(P)).then_inc(small_in, 16)
            sp.dma_start(half_col[:, :, :], col_b).then_inc(small_in, 16)
            sp.dma_start(bo_row[:, :], bo.partition_broadcast(P)).then_inc(small_in, 16)
            sp.dma_start(w_all[:, WQ:WO, :, :], weights[:, WQ:WO]).then_inc(qkv_in, 16)
            sp.wait_ge(tok_step, TOK_STEPS)
            store_pair(sp, 0)
            sp.wait_ge(rec_out, 16)
            load_hidden(sp, 0, 0)
            sp.dma_start(w_all[:, WO:12, :, :], weights[:, WO:12]).then_inc(rest_in, 16)

            def slot_dmas(slot):
                if slot.pair and slot.par == 0:
                    p_value = slot.at(lambda t: t // 2 + 1)
                    pixels = x[p_value] if slot.k is None else x[bass.ds(p_value, 1)].rearrange("o p x -> (o p) x")
                    sp.dma_start(tok_x[:, :], pixels).then_inc(tok_in, 16)
                if slot.front:
                    for ready, sem_, parts, stack, blocks in ((q3_ready, q_stacked, q_parts, q_stack, Q_BLOCKS),
                                                              (k3_ready, k_stacked, k_parts, k_stack, K_BLOCKS)):
                        wait(sp, ready, slot, lambda t: t + 1)
                        for b, part in enumerate(blocks):
                            sp.dma_start(stack[DH * b:DH * (b + 1), slot.par].rearrange("r h t -> r (h t)"),
                                         parts[:, part].rearrange("p m t -> p (m t)")).then_inc(sem_, 16)
                if slot.pair and slot.par == 1:
                    tok_wait(sp, slot, TOK_STEPS)
                    p_value = slot.at(lambda t: t // 2 + 1)
                    store_pair(sp, p_value)
                    wait(sp, rec_out, slot, lambda t: 16 * (t // 2 + 2))
                    load_hidden(sp, p_value, slot.at(lambda t: t + 1))
                if slot.front:
                    emptied(sp, slot, "MT")
                    sp.dma_start(q_stack[QK_ROWS:S2_ROWS, slot.par].rearrange("r h t -> r (h t)"), max_rows[:, :]).then_inc(max_stacked, 16)

            all_slots(sp, slot_dmas)

            with sp.Fori(0, IMAGES // 2) as k:
                for s, ready in ((0, out_even), (1, out_odd)):
                    sp.wait_ge(ready, k + 1)
                    sp.dma_start(out[bass.ds(2 * k + s, 1)].rearrange("o (i p) c -> p (o i) c", p=P),
                                 xo[:, bass.ds((2 * k + s) * IMG, IMG)].rearrange("p (i c) -> p i c", i=TILES))\
                      .then_inc(stored, 16)
            sp.wait_ge(stored, 16 * IMAGES)

        @block.gpsimd
        def _(pool):
            pool.memset(ident[:, :], 0.0).then_inc(pool_set, 1)
            pool.memset(ident_b[:, :], 0.0).then_inc(pool_set, 1)
            pool.memset(mask_qk[:, :], 0.0).then_inc(pool_set, 1)
            pool.memset(mask_kq[:, :], 0.0).then_inc(pool_set, 1)
            pool.wait_ge(pool_set, 4)
            for m in (ident, ident_b):
                pool.affine_select(out=m[:, :], in_=m[:, :], compare_op=ALU.not_equal, fill=1.0, base=0,
                                   pattern=[[-1, P]], channel_multiplier=1).then_inc(consts_set, 1)
            pool.affine_select(out=mask_qk[:, :], in_=mask_qk[:, :], compare_op=ALU.is_ge, fill=MASKED, base=0,
                               pattern=[[-1, P]], channel_multiplier=1).then_inc(consts_set, 1)
            pool.affine_select(out=mask_kq[:, :], in_=mask_kq[:, :], compare_op=ALU.is_ge, fill=MASKED, base=0,
                               pattern=[[1, P]], channel_multiplier=-1).then_inc(consts_set, 1)
            for par in range(2):
                pool.memset(v_pad[:, par], 0.0).then_inc(pads_set, 1)
            pool.wait_ge(consts_set, 7)
            pool.wait_ge(pads_set, 4)
            for par in range(2):
                pool.memset(k_stack[QK_ROWS:S2_ROWS, par, :, :], 1.0).then_inc(pads_set, 1)
            pool.wait_ge(pads_set, 6)
            ln_rstd(pool, BEFORE_FIRST, 0)

            def slot_pool(slot):
                if slot.pair and slot.par == 0:
                    wait(pool, tok_in, slot, lambda t: 16 * (t // 2 + 2))
                    tok_forward(pool, slot)
                if slot.pair and slot.par == 1:
                    small_wait(pool, slot, SMALL)
                    tok_backward(pool, slot)
                if slot.back:
                    ln_rstd(pool, slot, 1)
                if slot.next_front:
                    ln_rstd(pool, slot, 0)

            all_slots(pool, slot_pool)

            with pool.Fori(0, IMAGES // 2) as k:
                at = 2 * k * IMG
                pool.wait_ge(tanh_ready, 2 * k + 1)
                pool.tensor_tensor(xo[:, bass.ds(at, IMG)], xo[:, bass.ds(at, IMG)], hidden[:, bass.ds(at, IMG)],
                                   ALU.add).then_inc(out_even, 1)

        @block.scalar
        def _(act):
            tok_exps(act, FIRST_PAIR)
            ln_apply(act, BEFORE_FIRST, 0)

            def slot_act(slot):
                for u, job in enumerate(JOBS):
                    if slot.has(job):
                        if job == "XT1":
                            full(act, slot, job)
                            act.copy(xt1[:, :, :], bank(job).rearrange("p (k t) -> p k t", k=KT))\
                               .then_inc(stage_emptied[JOB_BANK[job]], 1)
                        elif job == "Q":
                            full(act, slot, job)
                            wait(act, q_stacked, slot, lambda t: 96 * t)
                            act.copy(q_parts[:, 0], bank(job).rearrange("p (m t) -> p m t", m=2)).then_inc(q1_ready, 1)
                        elif job == "K":
                            full(act, slot, job)
                            wait(act, k_stacked, slot, lambda t: 96 * t)
                            act.copy(k_parts[:, 0], bank(job).rearrange("p (m t) -> p m t", m=2)).then_inc(k1_ready, 1)
                            emptied(act, slot, "Q")
                            act.copy(q_parts[:, 1], q_rest[:, :].rearrange("p (m t) -> p m t", m=2)).then_inc(q2_ready, 1)
                        elif job == "V":
                            emptied(act, slot, "K")
                            act.copy(k_parts[:, 1], k_rest[:, :].rearrange("p (m t) -> p m t", m=2)).then_inc(k2_ready, 1)
                            if slot.k is None and slot.t == 0:
                                act.wait_ge(pads_set, 6)
                            full(act, slot, job)
                            src = bank(job).rearrange("p (i g s r) -> p i g s r", i=TILES, s=2, r=DH)
                            for i in range(TILES):
                                last = act.copy(v_pad[:, slot.par, i, :, 0:4:3, :], src[:, i])
                            last.then_inc(stage_emptied[JOB_BANK[job]], 1)
                        elif job == "XT2":
                            ln_apply(act, slot, 1)
                            full(act, slot, job)
                            act.copy(xt2[:, :, :], bank(job).rearrange("p (k t) -> p k t", k=KT))\
                               .then_inc(stage_emptied[JOB_BANK[job]], 1)
                        elif job in "FIG":
                            g = "FIG".index(job)
                            full(act, slot, job)
                            wait(act, c_ready, slot, lambda t: t - 1)
                            for m in range(KT):
                                last = act.activation(gate[:, g, m, :], bank(job)[:, m * S:(m + 1) * S], ACT.Tanh,
                                                      scale=0.5 if job in "FI" else 1.0, bias=gate_b[:, g, m:m + 1])
                            last.then_inc(stage_emptied[JOB_BANK[job]], 1)
                        elif job == "X":
                            full(act, slot, job)
                            act.copy(image(xo, slot, 2), bank(job)).then_inc(stage_emptied[JOB_BANK[job]], 1)
                        elif job == "MT":
                            full(act, slot, job)
                            wait(act, max_stacked, slot, lambda t: 16 * t)
                            rows = bank(job)[0:MAX_PARTS * HEADS, :].bitcast(BF16)[:, 0:S]
                            act.copy(max_rows[:, :], rows).then_inc(stage_emptied[JOB_BANK[job]], 1)
                    if job == "F" and slot.has("SUM"):
                        tok_exps(act, slot)
                    for n in S2_AT.get(u, ()) if slot.middle else ():
                        if n % 3 == 0:
                            wait(act, pv_done, slot, lambda t: PV_GROUPS * (t - 1) + n // 3 - 1)
                        wait(act, s2_full, slot, lambda t: S2_BANKS * (t - 1) + n + 1)
                        act.activation(probs[:, n % PROB_RING, :], s2[:, n % 2, :], ACT.Exp, scale=SCALE)\
                           .then_inc(probs_ready, 1)
                if slot.next_front:
                    ln_apply(act, slot, 0)

            all_slots(act, slot_act)

            with act.Fori(0, IMAGES) as k:
                act.wait_ge(pre_ready, k + 1)
                act.activation(xo[:, bass.ds(k * IMG, IMG)], xo[:, bass.ds(k * IMG, IMG)], ACT.Tanh)\
                   .then_inc(tanh_ready, 1)

        @block.vector
        def _(dve):
            dve.memset(same_image[:, :], 0.0)
            dve.memset(eps[:, :], EPS)
            dve.memset(neg_half[:, :], -0.5)
            dve.memset(ones_pad[:, :, :], 0.0).then_inc(dve_set, 1)
            dve.wait_ge(dve_set, 1)
            dve.memset(ones_pad[:, 0, 0:DH], 1.0)
            dve.memset(ones_pad[:, 1, DH:2 * DH], 1.0).then_inc(pads_set, 2)
            for i in range(2):
                dve.memset(same_image[64 * i:64 * (i + 1), 64 * i:64 * (i + 1)], 1.0).then_inc(consts_set, 1)
            dve.memset(spare[:, :], 0.0).then_inc(consts_set, 1)
            dve.memset(dots[:, 0:3], 0.0)
            dve.memset(logit_b[:, 1:2], 0.0)
            dve.memset(logit_b[:, 2:3], MASKED)
            for g, lv in enumerate((3, 3, 2, 1)):
                dve.memset(logit_s[:, 3 * g:3 * g + 3], 0.5 ** lv)
                dve.memset(band_s[:, 3 * g:3 * g + 3], 0.25 ** lv)
            dve.memset(c2[:, :, :], 0.0).then_inc(c_half, 1)
            dve.wait_ge(tok_in, 16)
            tok_forward(dve, FIRST_PAIR)
            dve.wait_ge(tokw_in, 16)
            dve.wait_ge(c_half, 1)
            tok_dots(dve, FIRST_PAIR)
            dve.wait_ge(small_in, 64)
            tok_logits(dve, FIRST_PAIR)
            for m in range(KT):
                dve.tensor_scalar(c2[:, m, :], c2[:, m, :], half_col[:, 3, m:m + 1], 2.0, ALU.add, ALU.mult)
            dve.tensor_scalar(gate_b[:, 0:2, :], half_col[:, 0:2, :], 0.5, None, ALU.mult)
            dve.tensor_copy(gate_b[:, 2, :], half_col[:, 2, :]).then_inc(c_ready, 1)
            tok_softmax(dve, FIRST_PAIR)
            small_wait(dve, FIRST_PAIR, SMALL)
            tok_backward(dve, FIRST_PAIR)
            dve.wait_ge(rest_in, 16)
            dve.tensor_scalar(w_all[:, UF:12, :, :], w_all[:, UF:12, :, :], 0.5, None, ALU.mult).then_inc(u_scaled, 1)
            dve.wait_ge(hidden_in, HIDDEN_DMAS)
            ln_stats(dve, BEFORE_FIRST, 0)
            ln_shift(dve, BEFORE_FIRST, 0)

            def slot_dve(slot):
                for u, job in enumerate(JOBS):
                    if slot.has(job):
                        if job == "WO":
                            full(dve, slot, job)
                            h = image(hidden, slot, 2)
                            dve.tensor_tensor(h, h, bank(job), ALU.add).then_inc(stage_emptied[JOB_BANK[job]], 1)
                            emptied(dve, slot, job)
                            ln_stats(dve, slot, 1)
                        elif job == "Q":
                            wait(dve, q1_ready, slot, lambda t: t + 1)
                            dve.tensor_tensor(q_rest[:, :], bank(job), q_parts[:, 0].rearrange("p m t -> p (m t)"),
                                              ALU.subtract).then_inc(stage_emptied[JOB_BANK[job]], 1)
                        elif job == "K":
                            wait(dve, k1_ready, slot, lambda t: t + 1)
                            dve.tensor_tensor(k_rest[:, :], bank(job), k_parts[:, 0].rearrange("p m t -> p (m t)"),
                                              ALU.subtract).then_inc(stage_emptied[JOB_BANK[job]], 1)
                            wait(dve, q2_ready, slot, lambda t: t + 1)
                            dve.tensor_tensor(q_parts[:, 2].rearrange("p m t -> p (m t)"), q_rest[:, :],
                                              q_parts[:, 1].rearrange("p m t -> p (m t)"), ALU.subtract)\
                               .then_inc(q3_ready, 1)
                        elif job == "V":
                            wait(dve, k2_ready, slot, lambda t: t + 1)
                            dve.tensor_tensor(k_parts[:, 2].rearrange("p m t -> p (m t)"), k_rest[:, :],
                                              k_parts[:, 1].rearrange("p m t -> p (m t)"), ALU.subtract)\
                               .then_inc(k3_ready, 1)
                        elif job == "SUM":
                            tok_logits(dve, slot)
                        elif job == "G":
                            f, i, g = (gate[:, n].rearrange("p m t -> p (m t)") for n in range(3))
                            c = c2[:, :, :].rearrange("p m t -> p (m t)")
                            emptied(dve, slot, "I")
                            dve.scalar_tensor_tensor(out=f, in0=f, scalar=1.0, in1=c, op0=ALU.add, op1=ALU.mult)
                            emptied(dve, slot, "G")
                            dve.scalar_tensor_tensor(out=i, in0=i, scalar=1.0, in1=g, op0=ALU.add, op1=ALU.mult)\
                               .then_inc(c_half, 1)
                            wait(dve, c_half, slot, lambda t: t)
                            dve.scalar_tensor_tensor(out=c, in0=f, scalar=0.5, in1=i, op0=ALU.mult, op1=ALU.add)\
                               .then_inc(c_ready, 1)
                    if job == "XT1" and slot.back:
                        ln_shift(dve, slot, 1)
                    if job == "V" and slot.has("SUM"):
                        tok_dots(dve, slot)
                    if job == "F" and slot.has("SUM"):
                        tok_softmax(dve, slot)
                    for n in S1_AT.get(u, ()) if slot.front else ():
                        wait(dve, s1_full, slot, lambda t: S1_BANKS * t + n + 1)
                        if n < 4:
                            src, dst = s1[:, n % 2, :].rearrange("p (h k) -> p h k", h=4), neg_max[:, 0, 4 * n:4 * n + 4]
                        else:
                            src = s1[:, n % 2, :].rearrange("p (h k) -> p h k", h=2)
                            dst = neg_max[:, 1, 2 * (n - 4):2 * (n - 4) + 2]
                        dve.tensor_reduce(dst, src, AX_X, ALU.max, negate=True).then_inc(s1_emptied, 1)
                    if slot.middle and PV_AT.get(u - 1) in (1, 3):
                        half = PV_AT[u - 1] // 2
                        wait(dve, pv_done, slot, lambda t: PV_GROUPS * (t - 1) + 2 * half + 2)
                        dve.reciprocal(row_inv[:, half], pv[:, half, 1]).then_inc(inv_ready, 1)
                        wait(dve, inv_ready, slot, lambda t: 2 * (t - 1) + half + 1)
                        dve.tensor_tensor(attn_t[:, half], pv[:, half, 0], row_inv[:, half], ALU.mult)\
                           .then_inc(attn_ready, 1)
                    if job == "X" and slot.front:
                        wait(dve, s1_emptied, slot, lambda t: S1_BANKS * (t + 1))
                        dve.tensor_copy(neg_max_parts[:, :, 0, :], neg_max[:, :, :]).then_inc(max_part1, 1)
                        wait(dve, max_part1, slot, lambda t: t + 1)
                        dve.tensor_tensor(neg_max_parts[:, :, 1, :], neg_max[:, :, :], neg_max_parts[:, :, 0, :],
                                          ALU.subtract).then_inc(max_parts_ready, 1)
                if slot.next_front:
                    wait(dve, hidden_in, slot, lambda t: HIDDEN_DMAS * ((t + 1) // 2 + 1))
                    ln_stats(dve, slot, 0)
                    ln_shift(dve, slot, 0)

            all_slots(dve, slot_dve)

            dve.wait_ge(stage_full[0], jobs_before(SLOTS - 1, "X") + 2)
            dve.tensor_tensor(cu[:, :, :], stage[:, 0, :].rearrange("p (i c) -> p i c", i=TILES),
                              bo_row[:, :].unsqueeze(1).to_broadcast([P, TILES, D]), ALU.add).then_inc(cu_ready, 1)
            dve.wait_ge(cu_ready, 1)
            dve.wait_ge(stage_emptied[0], jobs_before(SLOTS - 1, "X") + 1)
            flat_cu = cu[:, :, :].rearrange("p i c -> p (i c)")

            def pre(at):
                dve.tensor_tensor(xo[:, at], xo[:, at], flat_cu, ALU.add).then_inc(pre_ready, 1)

            pre(slice(0, IMG))
            pre(slice(IMG, 2 * IMG))

            def finish_odd(k):
                at = bass.ds((2 * k + 1) * IMG, IMG)
                dve.wait_ge(tanh_ready, 2 * k + 2)
                dve.tensor_tensor(xo[:, at], xo[:, at], hidden[:, at], ALU.add).then_inc(out_odd, 1)

            with dve.Fori(0, IMAGES // 2 - 1) as k:
                pre(bass.ds((2 * k + 2) * IMG, IMG))
                pre(bass.ds((2 * k + 3) * IMG, IMG))
                finish_odd(k)
            last = slice((IMAGES - 1) * IMG, IMAGES * IMG)
            dve.wait_ge(tanh_ready, IMAGES)
            dve.tensor_tensor(xo[:, last], xo[:, last], hidden[:, last], ALU.add).then_inc(out_odd, 1)

        @block.tensor
        def _(pe):
            pe.wait_ge(consts_set, 7)
            pe.wait_ge(dots_done, DOTS)
            tok_sum_matmul(pe)

            def begin(slot, job):
                wait(pe, stage_emptied[JOB_BANK[job]], slot, lambda t: jobs_before(t, job))

            def transposes(job, xn):
                out4 = bank(job).rearrange("p (k t) -> p k t", k=KT)
                for i in range(TILES):
                    for k in range(KT):
                        last = pe.transpose(out4[:, k, i * P:(i + 1) * P], xn[:, i, k * P:(k + 1) * P], ident[:, :])
                last.then_inc(stage_full[JOB_BANK[job]], 1)

            def product(dst, terms):
                n = len(terms) * KT
                for a, (lhs, rhs) in enumerate(terms):
                    for k in range(KT):
                        last = pe.matmul(dst, lhs(k), rhs(k), start=(a == 0 and k == 0), stop=(a * KT + k == n - 1))
                return last

            def by_feature(job, *pairs):
                for m in range(2):
                    cols = slice(m * P, (m + 1) * P)
                    last = product(bank(job)[:, m * S:(m + 1) * S],
                                   [(lambda k, w=w, c=cols: w_all[:, w, k, c], lambda k, b=b: b[:, k, :]) for w, b in pairs])
                last.then_inc(stage_full[JOB_BANK[job]], 1)

            def by_token(b, w, xt):
                for i in range(TILES):
                    last = product(stage[:, b, i * D:(i + 1) * D],
                                   [(lambda k, i=i: xt[:, k, i * P:(i + 1) * P], lambda k: w_all[:, w, k, :])])
                last.then_inc(stage_full[b], 1)

            def job_matmuls(slot, job):
                if job == "WO":
                    begin(slot, job)
                    wait(pe, attn_ready, slot, lambda t: 2 * (t - 1))
                    if slot.k is not None and slot.par == 0:
                        pe.wait_ge(rest_in, 16)
                        pe.wait_ge(u_scaled, 1)
                    by_token(JOB_BANK[job], WO, attn_t)
                elif job == "XT1":
                    begin(slot, job)
                    wait(pe, xn_ready[0], slot, lambda t: t + 1)
                    transposes(job, xn1)
                elif job in "QK":
                    begin(slot, job)
                    if job == "Q":
                        emptied(pe, slot, "XT1")
                    if slot.k is None and slot.t == 0:
                        pe.wait_ge(qkv_in, 16)
                    by_feature(job, (WQ if job == "Q" else WK, xt1))
                elif job == "V":
                    begin(slot, job)
                    by_token(JOB_BANK[job], WV, xt1)
                elif job == "SUM":
                    begin(slot, job)
                    wait(pe, dots_done, slot, lambda t: DOTS * (t // 2 + 2))
                    tok_sum_matmul(pe)
                elif job == "XT2":
                    begin(slot, job)
                    wait(pe, xn_ready[1], slot, lambda t: t - 1)
                    transposes(job, xn2)
                elif job in "FIG":
                    begin(slot, job)
                    if job == "F":
                        emptied(pe, slot, "XT2")
                        wait(pe, c_ready, slot, lambda t: t - 1)
                    g = "FIG".index(job)
                    by_feature(job, (WF + g, xt2), (UF + g, c2))
                elif job == "X":
                    begin(slot, job)
                    by_token(JOB_BANK[job], WX, xt2)
                elif job == "MT":
                    begin(slot, job)
                    wait(pe, max_parts_ready, slot, lambda t: t + 1)
                    rows = bank(job)[0:MAX_PARTS * HEADS, :].bitcast(BF16)
                    for i in range(TILES):
                        last = pe.transpose(rows[:, i * P:(i + 1) * P],
                                            neg_max_parts[:, i].rearrange("p a h -> p (a h)"), ident_b[:, :])
                    last.then_inc(stage_full[JOB_BANK[job]], 1)

            def max_scores(slot, n):
                if n == 0:
                    wait(pe, q_stacked, slot, lambda t: 96 * (t + 1))
                    wait(pe, k_stacked, slot, lambda t: 96 * (t + 1))
                wait(pe, s1_emptied, slot, lambda t: S1_BANKS * t + n - 1)
                dst = s1[:, n % 2, :]
                heads, keys, i = (range(4 * n, 4 * n + 4), P, 0) if n < 4 else (range(2 * (n - 4), 2 * (n - 4) + 2), S, 1)
                by_head = dst.rearrange("p (h k) -> p h k", k=keys)
                diag = by_head[:, :, keys - P:keys]
                pe.matmul(diag, ident_b[:, :], mask_qk[:, :].unsqueeze(1).to_broadcast([P, len(heads), P]),
                          start=True, stop=False, skip_group_check=True)
                for m, h in enumerate(heads):
                    last = pe.matmul(by_head[:, m, :], q_stack[0:QK_ROWS, slot.par, h, i * P:(i + 1) * P],
                                     k_stack[0:QK_ROWS, slot.par, h, 0:keys], start=False, stop=True,
                                     skip_group_check=True)
                last.then_inc(s1_full, 1)

            def place(h):
                return 2 * (h % (HEADS // 2)) + h // (HEADS // 2)

            def group_heads(g):
                return [8 * (g // 2) + 2 * j + g % 2 for j in range(4)]

            def exp_scores(slot, n):
                g, part = divmod(n, 3)
                par = 1 - slot.par
                if n == 0:
                    wait(pe, max_stacked, slot, lambda t: 16 * t)
                    if slot.k is None:
                        pe.wait_ge(pads_set, 6)
                wait(pe, probs_ready, slot, lambda t: S2_BANKS * (t - 1) + n - 1)
                heads = group_heads(g)[2 * part:2 * part + 2] if part < 2 else group_heads(g)
                i, queries = (0, S) if part < 2 else (1, P)
                by_head = s2[:, n % 2, :].rearrange("p (h q) -> p h q", q=queries)
                pe.matmul(by_head[:, :, 0:P], ident_b[:, :], mask_kq[:, :].unsqueeze(1).to_broadcast([P, len(heads), P]),
                          start=True, stop=False, skip_group_check=True)
                for m, h in enumerate(heads):
                    last = pe.matmul(by_head[:, m, :], k_stack[0:S2_ROWS, par, place(h), i * P:(i + 1) * P],
                                     q_stack[0:S2_ROWS, par, place(h), S - queries:S], start=False, stop=True,
                                     skip_group_check=True)
                last.then_inc(s2_full, 1)

            def times_v(slot, g):
                half, which = divmod(g, 2)
                par = 1 - slot.par
                wait(pe, probs_ready, slot, lambda t: S2_BANKS * (t - 1) + 3 * (g + 1))
                if which == 0:
                    wait(pe, attn_ready, slot, lambda t: 2 * (t - 1) - 1 + half)
                for values in (True, False):
                    for i, queries in ((0, S), (1, P)):
                        for j, h in enumerate(group_heads(g)):
                            b = (3 * g + (j // 2 if i == 0 else 2)) % PROB_RING
                            m = j % 2 if i == 0 else j
                            if values:
                                lhs = v_pad[:, par, i, h // 2, 2 * which:2 * which + 2, :].rearrange("p a r -> p (a r)")
                            else:
                                lhs = ones_pad[:, which, :]
                            last = pe.matmul(pv[32 * j:32 * (j + 1), half, 0 if values else 1, S - queries:S], lhs,
                                             probs[:, b, m * queries:(m + 1) * queries],
                                             start=(values and which == 0 and i == 0), stop=(which == 1 and i == 1),
                                             skip_group_check=True)
                last.then_inc(pv_done, 1)

            def slot_pe(slot):
                for u, job in enumerate(JOBS):
                    if slot.has(job):
                        job_matmuls(slot, job)
                    for n in S1_AT.get(u, ()) if slot.front else ():
                        max_scores(slot, n)
                    for n in S2_AT.get(u, ()) if slot.middle else ():
                        exp_scores(slot, n)
                    if slot.middle and u in PV_AT:
                        times_v(slot, PV_AT[u])

            all_slots(pe, slot_pe)

            pe.wait_ge(stage_emptied[0], jobs_before(SLOTS - 1, "X") + 1)
            pe.wait_ge(c_ready, IMAGES + 1)
            by_token(0, UX, c2)


def _lay_out(inputs):
    a = {k: np.asarray(v) for k, v in inputs.items()}

    def tiles(w):
        return w.reshape(KT, P, D).transpose(1, 0, 2)

    def by_row_of_head(w):
        return w.reshape(D, 2, HEADS // 2, DH).transpose(0, 1, 3, 2).reshape(D, D)

    mats = [by_row_of_head(a["L0_attn_Wq"].T), by_row_of_head(a["L0_attn_Wk"].T), a["L0_attn_Wv"].T, a["L0_attn_Wo"].T]
    mats += [a["L0_ffn_" + n].T for n in ("wf", "wi", "wc", "wo", "uf", "ui", "uc", "uo")]
    weights = np.stack([tiles(m) for m in mats], axis=1)

    vhd = [1, 0, 2]
    parts = []
    for lv, name in ((1, "Wd3"), (2, "Wd2"), (3, "Wd1")):
        rows, cols = (S >> lv) // 32, (D >> lv) // 2
        w = a["L0_tok_" + name].reshape(3, 32, rows, 2, cols, 3)[vhd][..., vhd]
        parts.append(w.transpose(1, 3, 5, 0, 2, 4).reshape(64, 9 * BAND[lv - 1]))
    parts.append(a["L0_tok_Wa"].reshape(32, 1, 2, 16).transpose(0, 2, 1, 3).reshape(64, BAND[2]))
    tok_w = np.concatenate(parts, axis=1)
    tok_w = np.concatenate([tok_w, tok_w], axis=0)
    tok_b = np.concatenate([a["L0_tok_ba"]] + [a["L0_tok_" + n][vhd] for n in ("bd1", "bd2", "bd3")])

    x = a["x"].reshape(PAIRS, 2, S // BR, BR, 2, BC).transpose(0, 1, 2, 4, 3, 5).reshape(PAIRS, P, XW)
    col_b = np.stack([a["L0_ffn_" + n].reshape(KT, P).T for n in ("bf", "bi", "bc", "in_c")], axis=1)
    arrays = {"x_in": x, "weights_in": weights, "tok_w_in": tok_w, "tok_b_in": tok_b, "col_b_in": col_b,
              "bo_in": a["L0_ffn_bo"]}
    return {k: np.ascontiguousarray(v) for k, v in arrays.items()}


def kernel(**inputs):
    import concourse.bacc as bacc
    from concourse.bass_utils import run_bass_kernel_spmd

    nc = bacc.Bacc("TRN2", target_bir_lowering=False, num_devices=1)
    arrays = _lay_out(inputs)
    args = [nc.dram_tensor(k, v.shape, mybir.dt.from_np(v.dtype), kind="ExternalInput").ap() for k, v in arrays.items()]
    out = nc.dram_tensor("out", (IMAGES, S, D), F32, kind="ExternalOutput").ap()
    scratch = nc.dram_tensor("scratch", (PAIRS, P, XW), F32, kind="Internal").ap()
    build(nc, *args, out, scratch)
    result = run_bass_kernel_spmd(nc, [arrays], core_ids=[0])
    return result.results[0]["out"]
```

```python
from contextlib import ExitStack

import numpy as np

import concourse.bass as bass
from concourse import mybir

F32 = mybir.dt.float32
F32R = mybir.dt.float32r
BF16 = mybir.dt.bfloat16
ALU = mybir.AluOpType
ACT = mybir.ActivationFunctionType
AX_X = mybir.AxisListType.X

P = 128
IMAGES = 16
S = 256
D = 256
HEADS = 16
DH = D // HEADS
TILES = S // P
KT = D // P
IMG = TILES * D
EPS = 1e-5
SCALE = DH ** -0.5
MASKED = -1e30

Q_BLOCKS = (0, 0, 1, 1, 0, 2)
K_BLOCKS = (0, 1, 0, 1, 2, 0)
QK_ROWS = len(Q_BLOCKS) * DH
MAX_PARTS = 2
S2_ROWS = QK_ROWS + MAX_PARTS

PAIRS = IMAGES // 2
BR, BC = 8, 128
XW = BR * BC
LEVELS = 3
BAND = [XW >> (2 * lv) for lv in range(1, LEVELS + 1)]
TOK_FWD, TOK_SCALE, TOK_INV = 12, 4, 12
TOK_STEPS = TOK_FWD + TOK_SCALE + TOK_INV
GROUPS = 4
LOGITS = 3 * GROUPS
W_OFF = {1: 0, 2: 9 * BAND[0], 3: 9 * (BAND[0] + BAND[1])}
W_A = 9 * sum(BAND)
W_ALL = W_A + BAND[2]

SPLIT = WQ, WK, WV, WF, WI, WC, WX = range(7)
WHOLE = WO, UF, UI, UC, UX = range(5)
RING = 8

S1_BANKS = 12
S2_BANKS = 12
PROB_RING = 6
PV_GROUPS = 4

PE_ORDER = """XT1 MT Q K S2_0 WO S2_1 S2_2 V PV_0 S2_3 S2_4 SUM S2_5 XT2 S2_6 S1_0 S2_7 PV_1 S1_1 F S2_8 S1_2 S2_9 PV_2
    I S1_3 G S1_4 S1_5 S2_10 S2_11 S1_6 X S1_7 S1_8 S1_9 PV_3 S1_10 S1_11""".split()
ACT_ORDER = """XT1 MT Q K Q2 E_0 WO K2 E_1 E_2 V E_3 E_4 LN2 SUM E_5 EXP3 XT2 E_6 E_7 E_8 HALF_0 E_9 F G I E_10 X E_11
    LN1 HALF_1""".split()
DVE_ORDER = """NEG XT1 HALF_1' Q K DOTS_0 DOTS_1 Q3 WO STATS2 K3 DOTS_2 DOTS_3 DOTS_4 LOGITS SHIFT2 SOFTMAX M_0 XT2 M_1
    M_2 STATS1 HALF_0 M_3 C_0 M_4 M_5 C_1 M_6 M_7 M_8 SHIFT1 M_9 M_10 M_11""".split()
POOL_ORDER = """FWD_0 FWD_1 FWD_2 FWD_3 BWD_0 BWD_1 BWD_2 BWD_3 FWD_4 FWD_5 FWD_6 FWD_7 FWD_8 FWD_9 FWD_10 FWD_11 BWD_4
    BWD_5 BWD_6 BWD_7 BWD_8 BWD_9 BWD_10 BWD_11 BWD_12 BWD_13 BWD_14 BWD_15 RSTD2 RSTD1""".split()
SP_ORDER = """MT P_0 P_1 P_2 SPILL PAIR""".split()
JOB_BANK = {"XT1": 0, "MT": 1, "Q": 0, "K": 1, "WO": 0, "V": 0, "SUM": 0, "XT2": 1, "F": 0, "I": 1, "G": 0, "X": 1}
LATE = "'"
FRONT, BACK = ("XT1", "Q", "K", "V"), ("WO", "XT2", "F", "I", "G", "X")

FIRST_LOOPED, LOOPS = 4, 5
SLOTS = IMAGES + 2


def runs(t, job):
    if job == "SUM":
        return t >= 0 and t % 2 == 0 and t // 2 + 1 < PAIRS
    if job == "MT":
        return 1 <= t <= IMAGES
    return 0 <= t < IMAGES if job in FRONT else 2 <= t < SLOTS


def job_number(bank, of_slot=None, of_job=None):
    n = 1 if bank == JOB_BANK["SUM"] else 0
    for t in range(SLOTS + 1):
        for step in PE_ORDER:
            job, at = step.rstrip(LATE), t - step.endswith(LATE)
            if job in JOB_BANK and JOB_BANK[job] == bank:
                if (at, job) == (of_slot, of_job):
                    return n
                n += runs(at, job)
    return n


def jobs_before(t, job):
    return job_number(JOB_BANK[job], t, job)


class Slot:

    def __init__(self, t, k=None):
        self.t, self.k = t, k
        self.par = t % 2
        looped = k is not None
        self.front = looped or 0 <= t < IMAGES
        self.middle = looped or 1 <= t <= IMAGES
        self.back = looped or 2 <= t < SLOTS
        self.pair = looped or t >= 0 and t // 2 + 1 < PAIRS
        self.next_front = looped or 0 <= t < IMAGES - 1

    def has(self, job):
        if job == "SUM":
            return self.pair and self.par == 0
        if job == "MT":
            return self.middle
        return self.front if job in FRONT else self.back

    def steps(self, order):
        before = Slot(self.t - 1, self.k)
        for step in order:
            name, _, n = step.rstrip(LATE).partition("_")
            yield name, int(n or 0), before if step.endswith(LATE) else self

    def at(self, count):
        if self.k is None:
            return count(self.t)
        return self.k * (count(self.t + 2) - count(self.t)) + count(self.t)


def wait(eng, sem, slot, count):
    if slot.k is None and count(slot.t) <= 0:
        return
    assert count(slot.t) > 0
    eng.wait_ge(sem, slot.at(count))


def all_slots(eng, body):
    for t in range(FIRST_LOOPED):
        body(Slot(t))
    with eng.Fori(0, LOOPS) as k:
        for s in range(2):
            body(Slot(FIRST_LOOPED + s, k))
    for t in range(FIRST_LOOPED + 2 * LOOPS, SLOTS + 1):
        body(Slot(t))


def build(nc, x, weights, tok_w, tok_b, col_b, bo, halves, out, scratch, spill):
    ctx = ExitStack()
    with ctx:
        def sb(name, shape, dt=F32):
            return ctx.enter_context(nc.sbuf_tensor(name, shape, dt))

        def ps(name, shape):
            return ctx.enter_context(nc.psum_tensor(name, shape, F32))

        def sem(name):
            return ctx.enter_context(nc.semaphore(name))

        hidden = sb("hidden", [P, RING * IMG])
        xo = sb("xo", [P, IMAGES * IMG])
        w_hi = sb("w_hi", [P, len(SPLIT), KT, D], F32R)
        w_lo = sb("w_lo", [P, len(SPLIT), KT, D], F32R)
        w_all = sb("w_all", [P, len(WHOLE), KT, D])
        w_raw = xo[:, RING * IMG:(RING + len(SPLIT)) * IMG].rearrange("p (w k c) -> p w k c", w=len(SPLIT), k=KT)
        q_stack = sb("q_stack", [P, 2, HEADS, S], BF16)
        k_stack = sb("k_stack", [P, 2, HEADS, S], BF16)
        q_parts = sb("q_parts", [P, 3, 2, S], BF16)
        k_parts = sb("k_parts", [P, 3, 2, S], BF16)
        q_rest = sb("q_rest", [P, 2 * S])
        k_rest = sb("k_rest", [P, 2 * S])
        v_pad = sb("v_pad", [P, 2, TILES, HEADS // 2, 4, DH])
        xn1 = sb("xn1", [P, TILES, D])
        xn2 = sb("xn2", [P, TILES, D])
        xt1 = [sb("xt1_hi", [P, KT, S], F32R), sb("xt1_lo", [P, KT, S], F32R)]
        xt2 = [sb("xt2_hi", [P, KT, S], F32R), sb("xt2_lo", [P, KT, S], F32R)]
        probs = sb("probs", [P, PROB_RING, 512])
        first_v = sb("first_v", [P, S])
        second_sum = sb("second_sum", [P, S])
        pair_v = sb("pair_v", [P, S])
        row_sum = sb("row_sum", [P, S])
        row_inv = sb("row_inv", [P, S])
        side = sb("side", [P, 2])
        low16, high16 = side[:, 0:1], side[:, 1:2]
        attn_t = sb("attn_t", [P, 2, S])
        gate = sb("gate", [P, 3, 2, S])
        c2 = sb("c2", [P, KT, S])
        neg_max = sb("neg_max", [P, TILES, HEADS])
        neg_max_parts = sb("neg_max_parts", [P, TILES, MAX_PARTS, HEADS], BF16)
        max_rows = sb("max_rows", [MAX_PARTS * HEADS, S], BF16)
        bn1 = sb("bn1", [P, TILES, 6])
        bn2 = sb("bn2", [P, TILES, 6])
        mv1 = sb("mv1", [P, TILES, 2])
        mv2 = sb("mv2", [P, TILES, 2])
        ln1 = sb("ln1", [P, 3, TILES])
        ln2 = sb("ln2", [P, 3, TILES])
        tok_x = sb("tok_x", [P, XW])
        tok_t = sb("tok_t", [P, XW])
        tok_c = {lv: sb(f"tok_c{lv}", [P, 4 * BAND[lv - 1]]) for lv in (1, 2, 3)}
        tok_weights = sb("tok_weights", [P, W_ALL])
        dots = sb("dots", [P, LOGITS])
        logit = sb("logit", [P, LOGITS])
        logit_b = sb("logit_b", [P, LOGITS])
        logit_s = sb("logit_s", [P, LOGITS])
        band_s = sb("band_s", [P, LOGITS])
        tok_max = sb("tok_max", [P, GROUPS])
        tok_sum = sb("tok_sum", [P, GROUPS])
        tok_exp = sb("tok_exp", [P, LOGITS])
        band_w = sb("band_w", [P, LOGITS])
        half_col = sb("half_col", [P, 4, KT])
        gate_b = sb("gate_b", [P, 3, KT])
        bo_row = sb("bo_row", [P, D])
        cu = sb("cu", [P, TILES, D])
        ident = sb("ident", [P, P])
        ident_b = sb("ident_b", [P, P], BF16)
        mask_qk = sb("mask_qk", [P, P], BF16)
        mask_kq = sb("mask_kq", [P, P], BF16)
        same_image = sb("same_image", [P, P])
        neg_half = sb("neg_half", [P, TILES])
        eps = sb("eps", [P, TILES])
        spare = sb("spare", [P, 1])

        stage = ps("stage", [P, 2, 512])
        s1 = ps("s1", [P, 2, 512])
        s2 = ps("s2", [P, 2, 512])
        pv = ps("pv", [P, 2, 2, S])

        consts_set = sem("consts_set")
        pool_set = sem("pool_set")
        pads_set = sem("pads_set")
        dve_set = sem("dve_set")
        tok_in = sem("tok_in")
        tokw_in = sem("tokw_in")
        small_in = sem("small_in")
        qkv_in = sem("qkv_in")
        rest_in = sem("rest_in")
        ffn_in = sem("ffn_in")
        w_hi_ready, w_lo_ready = sem("w_hi_ready"), sem("w_lo_ready")
        xt_hi_ready = [sem("xt1_hi_ready"), sem("xt2_hi_ready")]
        parts_ready, pair_ready, sum_ready, turned_ready = (sem(n) for n in ("parts_ready", "pair_ready", "sum_ready",
                                                                             "turned_ready"))
        spilled, reloaded = sem("spilled"), [sem("reloaded_even"), sem("reloaded_odd")]
        x_in = tok_in
        u_scaled = sem("u_scaled")
        tok_step = sem("tok_step")
        dots_done = sem("dots_done")
        tok_small = sem("tok_small")
        tok_exp_done = sem("tok_exp_done")
        rec_out = sem("rec_out")
        hidden_in = [sem("hidden_in_even"), sem("hidden_in_odd")]
        stage_full = [sem("stage_full0"), sem("stage_full1")]
        stage_emptied = [sem("stage_emptied0"), sem("stage_emptied1")]
        q1_ready, q2_ready, q3_ready = sem("q1_ready"), sem("q2_ready"), sem("q3_ready")
        k1_ready, k2_ready, k3_ready = sem("k1_ready"), sem("k2_ready"), sem("k3_ready")
        q_stacked = sem("q_stacked")
        k_stacked = sem("k_stacked")
        max_stacked = sem("max_stacked")
        s1_full, s1_emptied = sem("s1_full"), sem("s1_emptied")
        s2_full, probs_ready = sem("s2_full"), sem("probs_ready")
        max_part1, max_parts_ready = sem("max_part1"), sem("max_parts_ready")
        pv_done, inv_ready, attn_ready = sem("pv_done"), sem("inv_ready"), sem("attn_ready")
        bn_done = [sem("bn1_done"), sem("bn2_done")]
        mv_done = [sem("mv1_done"), sem("mv2_done")]
        eps_done = [sem("eps1_done"), sem("eps2_done")]
        rstd_done = [sem("rstd1_done"), sem("rstd2_done")]
        shift_done = [sem("shift1_done"), sem("shift2_done")]
        xn_ready = [sem("xn1_ready"), sem("xn2_ready")]
        c_half = sem("c_half")
        c_ready = sem("c_ready")
        cu_ready = sem("cu_ready")
        pre_ready, tanh_ready = sem("pre_ready"), sem("tanh_ready")
        out_even, out_odd = sem("out_even"), sem("out_odd")
        stored = sem("stored")

        block = ctx.enter_context(nc.Block())

        def full(eng, slot, job):
            wait(eng, stage_full[JOB_BANK[job]], slot, lambda t: jobs_before(t, job) + 1)

        def emptied(eng, slot, job):
            wait(eng, stage_emptied[JOB_BANK[job]], slot, lambda t: jobs_before(t, job) + 1)

        def bank(job):
            return stage[:, JOB_BANK[job], :]

        def residual(slot, back):
            return hidden[:, bass.ds(slot.at(lambda t: t - back) % RING * IMG, IMG)]

        def tok_wait(eng, slot, n):
            wait(eng, tok_step, slot, lambda t: TOK_STEPS * (t // 2 + 1) + n)

        def tok_forward(eng, slot, pieces=range(TOK_FWD)):
            for piece in pieces:
                lv, part = piece // 4 + 1, piece % 4
                src, n = (tok_x, tok_c[1], tok_c[2])[lv - 1], XW >> 2 * (lv - 1)
                h, c = n // 2, BC >> lv
                op = (ALU.add, ALU.subtract)[part % 2]
                at = slice(part % 2 * h, (part % 2 + 1) * h)
                if part < 2:
                    even = src[:, 0:n].rearrange("p (n two) -> p two n", two=2)
                    if lv > 1:
                        tok_wait(eng, slot, piece - part)
                    eng.tensor_tensor(tok_t[:, at], even[:, 0], even[:, 1], op).then_inc(tok_step, 1)
                else:
                    rows = tok_t[:, 0:n].rearrange("p (m two c) -> p two m c", two=2, c=c)
                    tok_wait(eng, slot, piece - part + 2)
                    eng.tensor_tensor(tok_c[lv][:, at].rearrange("p (m c) -> p m c", c=c), rows[:, 0], rows[:, 1],
                                      op).then_inc(tok_step, 1)

        def tok_backward(eng, slot, pieces=range(TOK_SCALE + TOK_INV)):
            for piece in pieces:
                if piece == 0:
                    n3 = BAND[2]
                    eng.tensor_tensor(tok_c[3][:, 0:n3], tok_c[3][:, 0:n3], band_w[:, 0:1].to_broadcast([P, n3]),
                                      ALU.mult).then_inc(tok_step, 1)
                elif piece < TOK_SCALE:
                    lv = TOK_SCALE - piece
                    n, g = BAND[lv - 1], GROUPS - lv
                    bands = tok_c[lv][:, n:4 * n].rearrange("p (b n) -> p b n", b=3)
                    wts = band_w[:, 3 * g:3 * g + 3].unsqueeze(2).to_broadcast([P, 3, n])
                    eng.tensor_tensor(bands, bands, wts, ALU.mult).then_inc(tok_step, 1)
                else:
                    lv, part = LEVELS - piece // 4 + 1, piece % 4
                    n = 4 * BAND[lv - 1]
                    h, c = n // 2, BC >> lv
                    op = (ALU.add, ALU.subtract)[part % 2]
                    if part < 2:
                        rows = tok_t[:, 0:n].rearrange("p (m two c) -> p two m c", two=2, c=c)
                        av = tok_c[lv][:, 0:h].rearrange("p (m c) -> p m c", c=c)
                        hd = tok_c[lv][:, h:n].rearrange("p (m c) -> p m c", c=c)
                        tok_wait(eng, slot, TOK_FWD + piece - part)
                        eng.tensor_tensor(rows[:, part], av, hd, op).then_inc(tok_step, 1)
                    else:
                        dst = tok_x if lv == 1 else tok_c[lv - 1]
                        cols = dst[:, 0:n].rearrange("p (n two) -> p two n", two=2)
                        tok_wait(eng, slot, TOK_FWD + piece - part + 2)
                        eng.tensor_tensor(cols[:, part - 2], tok_t[:, 0:h], tok_t[:, h:n], op).then_inc(tok_step, 1)

        DOTS = 10
        DOT_PIECES = ((0, 4), (4, 7), (7, 8), (8, 9), (9, 10))
        FIRST_PAIR = Slot(-2)

        def tok_dots(eng, slot, piece):
            if piece == 0:
                tok_wait(eng, slot, TOK_FWD)
            columns = [(0, 3, 0, BAND[2], W_A)]
            for lv in (3, 2, 1):
                n, g = 3 * BAND[lv - 1], GROUPS - lv
                columns += [(3 * g + j, lv, n // 3, n, W_OFF[lv] + j * n) for j in range(3)]
            for i in range(*DOT_PIECES[piece]):
                col, lv, first, n, off = columns[i]
                products = (tok_t, tok_x)[i % 2]
                if i >= 2:
                    wait(eng, dots_done, slot, lambda t: DOTS * (t // 2 + 1) + i - 1)
                eng.tensor_tensor_reduce(products[:, 0:n], tok_c[lv][:, first:first + n], tok_weights[:, off:off + n],
                                         1.0, 0.0, ALU.mult, ALU.add, dots[:, col:col + 1]).then_inc(dots_done, 1)

        SMALL = 7

        def small_wait(eng, slot, n):
            wait(eng, tok_small, slot, lambda t: SMALL * (t // 2 + 1) + n)

        def tok_logits(eng, slot):
            l3 = logit[:, :].rearrange("p (g j) -> p g j", j=3)
            if slot is FIRST_PAIR:
                eng.wait_ge(stage_full[JOB_BANK["SUM"]], 1)
            else:
                full(eng, slot, "SUM")
            eng.tensor_tensor(logit[:, :], bank("SUM")[:, 0:LOGITS], logit_s[:, :], ALU.mult)\
               .then_inc(stage_emptied[JOB_BANK["SUM"]], 1)
            if slot is FIRST_PAIR:
                eng.wait_ge(stage_emptied[JOB_BANK["SUM"]], 1)
            else:
                emptied(eng, slot, "SUM")
            eng.tensor_tensor(logit[:, :], logit[:, :], logit_b[:, :], ALU.add).then_inc(tok_small, 1)
            small_wait(eng, slot, 1)
            eng.tensor_reduce(tok_max[:, :], l3, AX_X, ALU.max).then_inc(tok_small, 1)
            small_wait(eng, slot, 2)
            eng.tensor_tensor(l3, l3, tok_max[:, :].unsqueeze(2).to_broadcast([P, GROUPS, 3]), ALU.subtract)\
               .then_inc(tok_small, 1)

        def tok_exps(eng, slot):
            small_wait(eng, slot, 3)
            eng.activation(tok_exp[:, :], logit[:, :], ACT.Exp).then_inc(tok_exp_done, 1)

        def tok_softmax(eng, slot):
            e3 = tok_exp[:, :].rearrange("p (g j) -> p g j", j=3)
            wait(eng, tok_exp_done, slot, lambda t: t // 2 + 2)
            eng.tensor_reduce(tok_sum[:, :], e3, AX_X, ALU.add).then_inc(tok_small, 1)
            small_wait(eng, slot, 4)
            eng.reciprocal(tok_max[:, :], tok_sum[:, :]).then_inc(tok_small, 1)
            small_wait(eng, slot, 5)
            eng.tensor_tensor(e3, e3, tok_max[:, :].unsqueeze(2).to_broadcast([P, GROUPS, 3]), ALU.mult)\
               .then_inc(tok_small, 1)
            small_wait(eng, slot, 6)
            eng.tensor_tensor(band_w[:, :], tok_exp[:, :], band_s[:, :], ALU.mult).then_inc(tok_small, 1)

        def tok_sum_matmul(eng):
            eng.matmul(bank("SUM")[:, 0:LOGITS], same_image[:, :], dots[:, :], start=True, stop=True)\
               .then_inc(stage_full[JOB_BANK["SUM"]], 1)

        LN = [(bn1, mv1, ln1, xn1), (bn2, mv2, ln2, xn2)]
        LN_COUNT = [lambda t: t + 2, lambda t: t - 1]

        def ln_stats(eng, slot, which):
            bn, mv, _, _ = LN[which]
            src = residual(slot, -1 if which == 0 else 2).rearrange("p (i c) -> p i c", i=TILES)
            eng.memset(spare[:, :], 0.0)
            for i in range(TILES):
                last = eng.bn_stats(bn[:, i, :], src[:, i, :])
            last.then_inc(bn_done[which], 1)
            wait(eng, bn_done[which], slot, LN_COUNT[which])
            eng.memset(spare[:, :], 0.0)
            for i in range(TILES):
                last = eng.bn_aggr(mv[:, i, :], bn[:, i, :])
            last.then_inc(mv_done[which], 1)

        def ln_rstd(eng, slot, which):
            _, mv, ln, _ = LN[which]
            wait(eng, mv_done[which], slot, LN_COUNT[which])
            eng.tensor_tensor(ln[:, 0, :], mv[:, :, 1], eps[:, :], ALU.add).then_inc(eps_done[which], 1)
            wait(eng, eps_done[which], slot, LN_COUNT[which])
            eng.tensor_tensor(ln[:, 1, :], ln[:, 0, :], neg_half[:, :], ALU.pow).then_inc(rstd_done[which], 1)

        def ln_shift(eng, slot, which):
            _, mv, ln, _ = LN[which]
            wait(eng, rstd_done[which], slot, LN_COUNT[which])
            eng.scalar_tensor_tensor(out=ln[:, 2, :], in0=mv[:, :, 0], scalar=-1.0, in1=ln[:, 1, :],
                                     op0=ALU.mult, op1=ALU.mult).then_inc(shift_done[which], 1)

        def ln_apply(eng, slot, which):
            _, _, ln, xn = LN[which]
            src = residual(slot, -1 if which == 0 else 2).rearrange("p (i c) -> p i c", i=TILES)
            wait(eng, shift_done[which], slot, LN_COUNT[which])
            for i in range(TILES):
                last = eng.activation(xn[:, i, :], src[:, i, :], ACT.Identity, scale=ln[:, 1, i:i + 1],
                                      bias=ln[:, 2, i:i + 1])
            last.then_inc(xn_ready[which], 1)

        BEFORE_FIRST = Slot(-1)

        def store_pair(sp, p_value):
            sp.dma_start(scratch[bass.ds(p_value, 1)].rearrange("o p x -> (o p) x"), tok_x[:, :]).then_inc(rec_out, 16)

        def load_hidden(sp, p_value, first_image):
            pair = scratch[bass.ds(p_value, 1)].rearrange("o (i b ch) (r c) -> (o i) b r ch c", i=2, ch=2, c=BC)
            for i in range(2):
                for tile in range(TILES):
                    blocks = P // BR
                    off = (first_image % RING + i) * IMG + tile * D
                    for ch in range(2):
                        sp.dma_start(hidden[:, bass.ds(off + ch * BC, BC)],
                                     pair[i, tile * blocks:(tile + 1) * blocks, :, ch, :]).then_inc(hidden_in[i], 16)

        HIDDEN_DMAS = TILES * 2 * 16

        @block.sync
        def _(sp):
            sp.dma_start(tok_x[:, :], x[0]).then_inc(tok_in, 16)
            sp.dma_start(tok_weights[:, :], tok_w).then_inc(tokw_in, 16)
            sp.dma_start(logit_b[:, 0:1], tok_b[0:1].partition_broadcast(P)).then_inc(small_in, 16)
            sp.dma_start(logit_b[:, 3:LOGITS], tok_b[1:10].partition_broadcast(P)).then_inc(small_in, 16)
            sp.dma_start(half_col[:, :, :], col_b).then_inc(small_in, 16)
            sp.dma_start(side[:, :], halves).then_inc(small_in, 16)
            sp.dma_start(bo_row[:, :], bo.partition_broadcast(P)).then_inc(small_in, 16)
            sp.dma_start(w_raw[:, WQ:WF], weights[:, WQ:WF]).then_inc(qkv_in, 16)
            sp.dma_start(w_raw[:, WF:], weights[:, WF:len(SPLIT)]).then_inc(ffn_in, 16)
            sp.wait_ge(tok_step, TOK_STEPS)
            store_pair(sp, 0)
            sp.wait_ge(rec_out, 16)
            load_hidden(sp, 0, 0)
            sp.dma_start(w_all[:, :, :, :], weights[:, len(SPLIT):]).then_inc(rest_in, 16)

            def slot_dmas(now):
                slot = now
                if slot.pair and slot.par == 0:
                    p_value = slot.at(lambda t: t // 2 + 1)
                    pixels = x[p_value] if slot.k is None else x[bass.ds(p_value, 1)].rearrange("o p x -> (o p) x")
                    sp.dma_start(tok_x[:, :], pixels).then_inc(tok_in, 16)
                for name, n, slot in now.steps(SP_ORDER):
                    if name == "MT" and slot.middle:
                        emptied(sp, slot, "MT")
                        sp.dma_start(q_stack[QK_ROWS:S2_ROWS, 1 - slot.par].rearrange("r h t -> r (h t)"),
                                     max_rows[:, :]).then_inc(max_stacked, 16)
                    if name == "P" and slot.front:
                        part = n
                        for ready, sem_, parts, stack, blocks in (
                                ((q1_ready, q2_ready, q3_ready)[part], q_stacked, q_parts, q_stack, Q_BLOCKS),
                                ((k1_ready, k2_ready, k3_ready)[part], k_stacked, k_parts, k_stack, K_BLOCKS)):
                            wait(sp, ready, slot, lambda t: t + 1)
                            for b in range(len(blocks)):
                                if blocks[b] == part:
                                    sp.dma_start(stack[DH * b:DH * (b + 1), slot.par].rearrange("r h t -> r (h t)"),
                                                 parts[:, part].rearrange("p m t -> p (m t)")).then_inc(sem_, 16)
                    if name == "SPILL" and slot.back and (slot.k is not None or slot.t - 2 < RING):
                        emptied(sp, slot, "WO")
                        sp.dma_start(spill[bass.ds(slot.at(lambda t: t - 2), 1)].rearrange("o p x -> (o p) x"),
                                     residual(slot, 2)).then_inc(spilled, 16)
                    if name == "PAIR" and slot.pair and slot.par == 1:
                        if slot.k is not None:
                            wait(sp, spilled, slot, lambda t: 16 * (t - 1))
                        tok_wait(sp, slot, TOK_STEPS)
                        p_value = slot.at(lambda t: t // 2 + 1)
                        store_pair(sp, p_value)
                        wait(sp, rec_out, slot, lambda t: 16 * (t // 2 + 2))
                        load_hidden(sp, p_value, slot.at(lambda t: t + 1))

            all_slots(sp, slot_dmas)

            def store_image(k, s, ready):
                sp.wait_ge(ready, k + 1)
                sp.dma_start(out[bass.ds((2 * k + s + RING) % IMAGES, 1)].rearrange("o (i p) c -> p (o i) c", p=P),
                             xo[:, bass.ds((2 * k + s + RING) % IMAGES * IMG, IMG)].rearrange("p (i c) -> p i c", i=TILES))\
                  .then_inc(stored, 16)

            def reload(k, s):
                sp.dma_start(hidden[:, bass.ds((2 * k + s) * IMG, IMG)],
                             spill[bass.ds(2 * k + s, 1)].rearrange("o p x -> (o p) x")).then_inc(reloaded[s], 16)

            for s, ready in ((0, out_even), (1, out_odd)):
                store_image(0, s, ready)
                reload(0, s)
            with sp.Fori(1, RING // 2) as k:
                for s, ready in ((0, out_even), (1, out_odd)):
                    store_image(k, s, ready)
                    sp.wait_ge(reloaded[s], 16 * k)
                    reload(k, s)
            with sp.Fori(RING // 2, IMAGES // 2) as k:
                for s, ready in ((0, out_even), (1, out_odd)):
                    store_image(k, s, ready)
            sp.wait_ge(stored, 16 * IMAGES)

        @block.gpsimd
        def _(pool):
            pool.memset(ident[:, :], 0.0).then_inc(pool_set, 1)
            pool.memset(ident_b[:, :], 0.0).then_inc(pool_set, 1)
            pool.memset(mask_qk[:, :], 0.0).then_inc(pool_set, 1)
            pool.memset(mask_kq[:, :], 0.0).then_inc(pool_set, 1)
            pool.wait_ge(pool_set, 4)
            for m in (ident, ident_b):
                pool.affine_select(out=m[:, :], in_=m[:, :], compare_op=ALU.not_equal, fill=1.0, base=0,
                                   pattern=[[-1, P]], channel_multiplier=1).then_inc(consts_set, 1)
            pool.affine_select(out=mask_qk[:, :], in_=mask_qk[:, :], compare_op=ALU.is_ge, fill=MASKED, base=0,
                               pattern=[[-1, P]], channel_multiplier=1).then_inc(consts_set, 1)
            pool.affine_select(out=mask_kq[:, :], in_=mask_kq[:, :], compare_op=ALU.is_ge, fill=MASKED, base=0,
                               pattern=[[1, P]], channel_multiplier=-1).then_inc(consts_set, 1)
            for par in range(2):
                pool.memset(v_pad[:, par], 1.0).then_inc(pads_set, 1)
            pool.wait_ge(consts_set, 7)
            pool.wait_ge(pads_set, 2)
            for par in range(2):
                pool.memset(k_stack[QK_ROWS:S2_ROWS, par, :, :], 1.0).then_inc(pads_set, 1)
            pool.wait_ge(pads_set, 4)
            for first, end, arrived in ((WQ, WF, qkv_in), (WF, len(SPLIT), ffn_in)):
                pool.wait_ge(arrived, 16)
                for w in range(first, end):
                    pool.wait_ge(w_hi_ready, w + 1)
                    pool.tensor_tensor(w_lo[:, w], w_raw[:, w], w_hi[:, w], ALU.subtract).then_inc(w_lo_ready, 1)
            ln_rstd(pool, BEFORE_FIRST, 0)

            def slot_pool(now):
                for name, n, slot in now.steps(POOL_ORDER):
                    if name == "FWD" and slot.pair and slot.par == 0:
                        if n == 0:
                            wait(pool, tok_in, slot, lambda t: 16 * (t // 2 + 2))
                        tok_forward(pool, slot, [n])
                    elif name == "BWD" and slot.pair and slot.par == 1:
                        if n == 0:
                            small_wait(pool, slot, SMALL)
                        tok_backward(pool, slot, [n])
                    elif name == "RSTD2" and slot.back:
                        ln_rstd(pool, slot, 1)
                    elif name == "RSTD1" and slot.next_front:
                        ln_rstd(pool, slot, 0)

            all_slots(pool, slot_pool)

            def finish_even(k):
                xo_at = bass.ds((2 * k + RING) % IMAGES * IMG, IMG)
                pool.tensor_tensor(xo[:, xo_at], xo[:, xo_at], hidden[:, bass.ds(2 * k % RING * IMG, IMG)], ALU.add)\
                    .then_inc(out_even, 1)

            with pool.Fori(0, RING // 2) as k:
                pool.wait_ge(tanh_ready, 2 * k + 1)
                finish_even(k)
            with pool.Fori(RING // 2, IMAGES // 2) as k:
                pool.wait_ge(reloaded[0], 16 * k + 16 - 8 * RING)
                pool.wait_ge(tanh_ready, 2 * k + 1)
                finish_even(k)

        @block.scalar
        def _(act):
            for first, end, arrived in ((WQ, WF, qkv_in), (WF, len(SPLIT), ffn_in)):
                act.wait_ge(arrived, 16)
                for w in range(first, end):
                    act.copy(w_hi[:, w], w_raw[:, w]).then_inc(w_hi_ready, 1)
            tok_exps(act, FIRST_PAIR)
            ln_apply(act, BEFORE_FIRST, 0)

            def slot_act(now):
                for name, n, slot in now.steps(ACT_ORDER):
                    if name == "XT1" and slot.front:
                        full(act, slot, "XT1")
                        act.copy(xt1[0][:, :, :], bank("XT1").rearrange("p (k t) -> p k t", k=KT))\
                           .then_inc(xt_hi_ready[0], 1)
                    elif name == "Q" and slot.front:
                        full(act, slot, "Q")
                        wait(act, q_stacked, slot, lambda t: 96 * t)
                        act.copy(q_parts[:, 0], bank("Q").rearrange("p (m t) -> p m t", m=2)).then_inc(q1_ready, 1)
                    elif name == "K" and slot.front:
                        full(act, slot, "K")
                        wait(act, k_stacked, slot, lambda t: 96 * t)
                        act.copy(k_parts[:, 0], bank("K").rearrange("p (m t) -> p m t", m=2)).then_inc(k1_ready, 1)
                    elif name == "Q2" and slot.front:
                        emptied(act, slot, "Q")
                        act.copy(q_parts[:, 1], q_rest[:, :].rearrange("p (m t) -> p m t", m=2)).then_inc(q2_ready, 1)
                    elif name == "K2" and slot.front:
                        emptied(act, slot, "K")
                        act.copy(k_parts[:, 1], k_rest[:, :].rearrange("p (m t) -> p m t", m=2)).then_inc(k2_ready, 1)
                    elif name == "V" and slot.front:
                        if slot.k is None and slot.t == 0:
                            act.wait_ge(pads_set, 4)
                        full(act, slot, "V")
                        src = bank("V").rearrange("p (i g s r) -> p i g s r", i=TILES, s=2, r=DH)
                        for i in range(TILES):
                            last = act.copy(v_pad[:, slot.par, i, :, 0:4:3, :], src[:, i])
                        last.then_inc(stage_emptied[JOB_BANK["V"]], 1)
                    elif name == "LN2" and slot.back:
                        ln_apply(act, slot, 1)
                    elif name == "XT2" and slot.back:
                        full(act, slot, "XT2")
                        act.copy(xt2[0][:, :, :], bank("XT2").rearrange("p (k t) -> p k t", k=KT))\
                           .then_inc(xt_hi_ready[1], 1)
                    elif name in ("F", "I", "G") and slot.back:
                        g = "FIG".index(name)
                        full(act, slot, name)
                        wait(act, c_ready, slot, lambda t: t - 1)
                        for m in range(KT):
                            last = act.activation(gate[:, g, m, :], bank(name)[:, m * S:(m + 1) * S], ACT.Tanh,
                                                  scale=0.5 if name in "FI" else 1.0, bias=gate_b[:, g, m:m + 1])
                        last.then_inc(stage_emptied[JOB_BANK[name]], 1)
                    elif name == "X" and slot.back:
                        full(act, slot, "X")
                        act.copy(xo[:, bass.ds(slot.at(lambda t: (t - 2) * IMG), IMG)], bank("X"))\
                           .then_inc(stage_emptied[JOB_BANK["X"]], 1)
                    elif name == "MT" and slot.middle:
                        full(act, slot, "MT")
                        wait(act, max_stacked, slot, lambda t: 16 * (t - 1))
                        rows = bank("MT")[0:MAX_PARTS * HEADS, :].bitcast(BF16)[:, 0:S]
                        act.copy(max_rows[:, :], rows).then_inc(stage_emptied[JOB_BANK["MT"]], 1)
                    elif name == "EXP3" and slot.has("SUM"):
                        tok_exps(act, slot)
                    elif name == "HALF" and slot.middle:
                        wait(act, pv_done, slot, lambda t: PV_GROUPS * (t - 1) + 2 * n + 2)
                        wait(act, attn_ready, slot, lambda t: 2 * (t - 1) + n)
                        act.activation(first_v[:, :], pv[:, n, 0], ACT.Copy, scale=low16)
                        act.activation(second_sum[:, :], pv[:, n, 1], ACT.Copy, scale=low16).then_inc(parts_ready, 1)
                    elif name == "LN1" and slot.next_front:
                        ln_apply(act, slot, 0)
                    elif name == "E" and slot.middle:
                        if n % 3 == 0:
                            wait(act, pv_done, slot, lambda t: PV_GROUPS * (t - 1) + n // 3 - 1)
                        wait(act, s2_full, slot, lambda t: S2_BANKS * (t - 1) + n + 1)
                        act.activation(probs[:, n % PROB_RING, :], s2[:, n % 2, :], ACT.Exp, scale=SCALE)\
                           .then_inc(probs_ready, 1)

            all_slots(act, slot_act)

            with act.Fori(0, IMAGES) as k:
                at = bass.ds((k + RING) % IMAGES * IMG, IMG)
                act.wait_ge(pre_ready, k + 1)
                act.activation(xo[:, at], xo[:, at], ACT.Tanh).then_inc(tanh_ready, 1)

        @block.vector
        def _(dve):
            dve.memset(same_image[:, :], 0.0)
            dve.memset(eps[:, :], EPS)
            dve.memset(spare[:, :], 0.0).then_inc(dve_set, 1)
            dve.wait_ge(dve_set, 1)
            for i in range(2):
                dve.memset(same_image[64 * i:64 * (i + 1), 64 * i:64 * (i + 1)], 1.0).then_inc(consts_set, 1)
            dve.memset(neg_half[:, :], -0.5).then_inc(consts_set, 1)
            dve.memset(dots[:, 0:3], 0.0)
            dve.memset(logit_b[:, 1:2], 0.0)
            dve.memset(logit_b[:, 2:3], MASKED)
            for g, lv in enumerate((3, 3, 2, 1)):
                dve.memset(logit_s[:, 3 * g:3 * g + 3], 0.5 ** lv)
                dve.memset(band_s[:, 3 * g:3 * g + 3], 0.25 ** lv)
            dve.memset(c2[:, :, :], 0.0).then_inc(c_half, 1)
            dve.wait_ge(tok_in, 16)
            tok_forward(dve, FIRST_PAIR)
            dve.wait_ge(tokw_in, 16)
            dve.wait_ge(c_half, 1)
            for piece in range(len(DOT_PIECES)):
                tok_dots(dve, FIRST_PAIR, piece)
            dve.wait_ge(small_in, 80)
            tok_logits(dve, FIRST_PAIR)
            for m in range(KT):
                dve.tensor_scalar(c2[:, m, :], c2[:, m, :], half_col[:, 3, m:m + 1], 2.0, ALU.add, ALU.mult)
            dve.tensor_scalar(gate_b[:, 0:2, :], half_col[:, 0:2, :], 0.5, None, ALU.mult)
            dve.tensor_copy(gate_b[:, 2, :], half_col[:, 2, :]).then_inc(c_ready, 1)
            tok_softmax(dve, FIRST_PAIR)
            small_wait(dve, FIRST_PAIR, SMALL)
            tok_backward(dve, FIRST_PAIR)
            dve.wait_ge(hidden_in[0], HIDDEN_DMAS)
            ln_stats(dve, BEFORE_FIRST, 0)
            ln_shift(dve, BEFORE_FIRST, 0)

            def slot_dve(now):
                if now.t == 1:
                    dve.wait_ge(rest_in, 16)
                    dve.tensor_scalar(w_all[:, UF:, :, :], w_all[:, UF:, :, :], 0.5, None, ALU.mult).then_inc(u_scaled, 1)
                for name, n, slot in now.steps(DVE_ORDER):
                    if name == "NEG" and slot.middle:
                        wait(dve, s1_emptied, slot, lambda t: S1_BANKS * t)
                        dve.tensor_copy(neg_max_parts[:, :, 0, :], neg_max[:, :, :]).then_inc(max_part1, 1)
                        wait(dve, max_part1, slot, lambda t: t)
                        dve.tensor_tensor(neg_max_parts[:, :, 1, :], neg_max[:, :, :], neg_max_parts[:, :, 0, :],
                                          ALU.subtract).then_inc(max_parts_ready, 1)
                    elif name == "WO" and slot.back:
                        full(dve, slot, "WO")
                        h = residual(slot, 2)
                        dve.tensor_tensor(h, h, bank("WO"), ALU.add).then_inc(stage_emptied[JOB_BANK["WO"]], 1)
                    elif name == "STATS2" and slot.back:
                        emptied(dve, slot, "WO")
                        ln_stats(dve, slot, 1)
                    elif name == "Q" and slot.front:
                        wait(dve, q1_ready, slot, lambda t: t + 1)
                        dve.tensor_tensor(q_rest[:, :], bank("Q"), q_parts[:, 0].rearrange("p m t -> p (m t)"),
                                          ALU.subtract).then_inc(stage_emptied[JOB_BANK["Q"]], 1)
                    elif name == "K" and slot.front:
                        wait(dve, k1_ready, slot, lambda t: t + 1)
                        dve.tensor_tensor(k_rest[:, :], bank("K"), k_parts[:, 0].rearrange("p m t -> p (m t)"),
                                          ALU.subtract).then_inc(stage_emptied[JOB_BANK["K"]], 1)
                    elif name == "Q3" and slot.front:
                        wait(dve, q2_ready, slot, lambda t: t + 1)
                        dve.tensor_tensor(q_parts[:, 2].rearrange("p m t -> p (m t)"), q_rest[:, :],
                                          q_parts[:, 1].rearrange("p m t -> p (m t)"), ALU.subtract)\
                           .then_inc(q3_ready, 1)
                    elif name == "K3" and slot.front:
                        wait(dve, k2_ready, slot, lambda t: t + 1)
                        dve.tensor_tensor(k_parts[:, 2].rearrange("p m t -> p (m t)"), k_rest[:, :],
                                          k_parts[:, 1].rearrange("p m t -> p (m t)"), ALU.subtract)\
                           .then_inc(k3_ready, 1)
                    elif name == "LOGITS" and slot.has("SUM"):
                        tok_logits(dve, slot)
                    elif name == "C" and slot.back:
                        f, i, g = (gate[:, a].rearrange("p m t -> p (m t)") for a in range(3))
                        c = c2[:, :, :].rearrange("p m t -> p (m t)")
                        if n == 0:
                            emptied(dve, slot, "F")
                            dve.scalar_tensor_tensor(out=f, in0=f, scalar=1.0, in1=c, op0=ALU.add, op1=ALU.mult)
                        else:
                            emptied(dve, slot, "I")
                            emptied(dve, slot, "G")
                            dve.scalar_tensor_tensor(out=i, in0=i, scalar=1.0, in1=g, op0=ALU.add, op1=ALU.mult)\
                               .then_inc(c_half, 1)
                            wait(dve, c_half, slot, lambda t: t)
                            dve.scalar_tensor_tensor(out=c, in0=f, scalar=0.5, in1=i, op0=ALU.mult, op1=ALU.add)\
                               .then_inc(c_ready, 1)
                    elif name in ("XT1", "XT2") and slot.has(name):
                        which = int(name[2]) - 1
                        xt = (xt1, xt2)[which]
                        wait(dve, xt_hi_ready[which], slot, lambda t: t + 1 - 2 * which)
                        dve.tensor_tensor(xt[1][:, :, :], bank(name).rearrange("p (k t) -> p k t", k=KT), xt[0][:, :, :],
                                          ALU.subtract).then_inc(stage_emptied[JOB_BANK[name]], 1)
                    elif name == "DOTS" and slot.has("SUM"):
                        tok_dots(dve, slot, n)
                    elif name == "SHIFT2" and slot.back:
                        ln_shift(dve, slot, 1)
                    elif name == "SOFTMAX" and slot.has("SUM"):
                        tok_softmax(dve, slot)
                    elif name == "STATS1" and slot.next_front:
                        wait(dve, hidden_in[1 - slot.par], slot, lambda t: HIDDEN_DMAS * ((t + 1) // 2 + 1))
                        ln_stats(dve, slot, 0)
                    elif name == "SHIFT1" and slot.next_front:
                        ln_shift(dve, slot, 0)
                    elif name == "M" and slot.front:
                        wait(dve, s1_full, slot, lambda t: S1_BANKS * t + n + 1)
                        if n < 4:
                            src, dst = s1[:, n % 2, :].rearrange("p (h k) -> p h k", h=4), neg_max[:, 0, 4 * n:4 * n + 4]
                        else:
                            src = s1[:, n % 2, :].rearrange("p (h k) -> p h k", h=2)
                            dst = neg_max[:, 1, 2 * (n - 4):2 * (n - 4) + 2]
                        dve.tensor_reduce(dst, src, AX_X, ALU.max, negate=True).then_inc(s1_emptied, 1)
                    elif name == "HALF" and slot.middle:
                        here = lambda t: 2 * (t - 1) + n + 1
                        wait(dve, parts_ready, slot, here)
                        dve.scalar_tensor_tensor(out=row_sum[:, :], in0=pv[:, n, 0], scalar=high16,
                                                 in1=second_sum[:, :], op0=ALU.mult, op1=ALU.add).then_inc(sum_ready, 1)
                        dve.scalar_tensor_tensor(out=pair_v[:, :], in0=pv[:, n, 1], scalar=high16,
                                                 in1=first_v[:, :], op0=ALU.mult, op1=ALU.add).then_inc(pair_ready, 1)
                        wait(dve, sum_ready, slot, here)
                        dve.memset(spare[:, :], 0.0)
                        dve.stream_shuffle(row_inv[:, :], row_sum[:, :], [*range(DH, 2 * DH), *range(DH)])\
                           .then_inc(turned_ready, 1)
                        wait(dve, turned_ready, slot, here)
                        dve.reciprocal(row_inv[:, :], row_inv[:, :]).then_inc(inv_ready, 1)
                        wait(dve, inv_ready, slot, here)
                        dve.tensor_tensor(attn_t[:, n], pair_v[:, :], row_inv[:, :], ALU.mult)\
                           .then_inc(attn_ready, 1)

            all_slots(dve, slot_dve)

            dve.wait_ge(stage_full[1], job_number(1) + 1)
            dve.tensor_tensor(cu[:, :, :], stage[:, 1, :].rearrange("p (i c) -> p i c", i=TILES),
                              bo_row[:, :].unsqueeze(1).to_broadcast([P, TILES, D]), ALU.add).then_inc(cu_ready, 1)
            dve.wait_ge(cu_ready, 1)
            dve.wait_ge(stage_emptied[1], job_number(1))
            flat_cu = cu[:, :, :].rearrange("p i c -> p (i c)")

            def pre(at):
                dve.tensor_tensor(xo[:, at], xo[:, at], flat_cu, ALU.add).then_inc(pre_ready, 1)

            def place_of(j):
                return bass.ds((j + RING) % IMAGES * IMG, IMG)

            def finish_odd(k):
                at = place_of(2 * k + 1)
                dve.wait_ge(tanh_ready, 2 * k + 2)
                dve.tensor_tensor(xo[:, at], xo[:, at], hidden[:, bass.ds((2 * k + 1) % RING * IMG, IMG)], ALU.add)\
                   .then_inc(out_odd, 1)

            pre(place_of(0))
            pre(place_of(1))
            with dve.Fori(0, RING // 2) as k:
                pre(place_of(2 * k + 2))
                pre(place_of(2 * k + 3))
                finish_odd(k)
            with dve.Fori(RING // 2, IMAGES // 2 - 1) as k:
                pre(place_of(2 * k + 2))
                pre(place_of(2 * k + 3))
                dve.wait_ge(reloaded[1], 16 * k + 16 - 8 * RING)
                finish_odd(k)
            dve.wait_ge(reloaded[1], 8 * RING)
            finish_odd(IMAGES // 2 - 1)

        @block.tensor
        def _(pe):
            pe.wait_ge(consts_set, 7)
            pe.wait_ge(dots_done, DOTS)
            tok_sum_matmul(pe)

            def begin(slot, job):
                wait(pe, stage_emptied[JOB_BANK[job]], slot, lambda t: jobs_before(t, job))

            def transposes(job, xn):
                out4 = bank(job).rearrange("p (k t) -> p k t", k=KT)
                for i in range(TILES):
                    for k in range(KT):
                        last = pe.transpose(out4[:, k, i * P:(i + 1) * P], xn[:, i, k * P:(k + 1) * P], ident[:, :])
                last.then_inc(stage_full[JOB_BANK[job]], 1)

            def product(dst, terms):
                for n, (lhs, rhs) in enumerate(terms):
                    last = pe.matmul(dst, lhs, rhs, start=(n == 0), stop=(n == len(terms) - 1))
                return last

            def split_terms(a, b, cols_a, cols_b):
                return [(a[i][:, k, cols_a], b[j][:, k, cols_b]) for k in range(KT) for i, j in ((0, 0), (1, 0), (0, 1))]

            def split_weight(w):
                return w_hi[:, w], w_lo[:, w]

            EVERY = slice(0, S)

            def by_feature(job, w, xt, u=None):
                for m in range(2):
                    cols = slice(m * P, (m + 1) * P)
                    terms = split_terms(split_weight(w), xt, cols, EVERY)
                    if u is not None:
                        terms += [(w_all[:, u, k, cols], c2[:, k, :]) for k in range(KT)]
                    last = product(bank(job)[:, m * S:(m + 1) * S], terms)
                last.then_inc(stage_full[JOB_BANK[job]], 1)

            def by_token(b, terms):
                for i in range(TILES):
                    last = product(stage[:, b, i * D:(i + 1) * D], terms(slice(i * P, (i + 1) * P)))
                last.then_inc(stage_full[b], 1)

            def whole_terms(xt, w):
                return lambda toks: [(xt[:, k, toks], w_all[:, w, k, :]) for k in range(KT)]

            def job_matmuls(slot, job):
                if job == "WO":
                    begin(slot, job)
                    wait(pe, attn_ready, slot, lambda t: 2 * (t - 1))
                    if slot.k is None and slot.t == 2:
                        pe.wait_ge(rest_in, 16)
                        pe.wait_ge(u_scaled, 1)
                    by_token(JOB_BANK[job], whole_terms(attn_t, WO))
                elif job == "XT1":
                    begin(slot, job)
                    wait(pe, xn_ready[0], slot, lambda t: t + 1)
                    transposes(job, xn1)
                elif job in "QK":
                    begin(slot, job)
                    if job == "Q":
                        emptied(pe, slot, "XT1")
                    if slot.k is None and slot.t == 0:
                        pe.wait_ge(w_lo_ready, len(SPLIT))
                    by_feature(job, WQ if job == "Q" else WK, xt1)
                elif job == "V":
                    begin(slot, job)
                    by_token(JOB_BANK[job], lambda toks: split_terms(xt1, split_weight(WV), toks, EVERY))
                elif job == "SUM":
                    begin(slot, job)
                    wait(pe, dots_done, slot, lambda t: DOTS * (t // 2 + 2))
                    tok_sum_matmul(pe)
                elif job == "XT2":
                    begin(slot, job)
                    wait(pe, xn_ready[1], slot, lambda t: t - 1)
                    transposes(job, xn2)
                elif job in "FIG":
                    begin(slot, job)
                    if job == "F":
                        emptied(pe, slot, "XT2")
                        wait(pe, c_ready, slot, lambda t: t - 1)
                    g = "FIG".index(job)
                    by_feature(job, WF + g, xt2, UF + g)
                elif job == "X":
                    begin(slot, job)
                    by_token(JOB_BANK[job], lambda toks: split_terms(xt2, split_weight(WX), toks, EVERY))
                elif job == "MT":
                    begin(slot, job)
                    wait(pe, max_parts_ready, slot, lambda t: t)
                    rows = bank(job)[0:MAX_PARTS * HEADS, :].bitcast(BF16)
                    for i in range(TILES):
                        last = pe.transpose(rows[:, i * P:(i + 1) * P],
                                            neg_max_parts[:, i].rearrange("p a h -> p (a h)"), ident_b[:, :])
                    last.then_inc(stage_full[JOB_BANK[job]], 1)

            def max_scores(slot, n):
                if n == 0:
                    wait(pe, q_stacked, slot, lambda t: 96 * (t + 1))
                    wait(pe, k_stacked, slot, lambda t: 96 * (t + 1))
                wait(pe, s1_emptied, slot, lambda t: S1_BANKS * t + n - 1)
                dst = s1[:, n % 2, :]
                heads, keys, i = (range(4 * n, 4 * n + 4), P, 0) if n < 4 else (range(2 * (n - 4), 2 * (n - 4) + 2), S, 1)
                by_head = dst.rearrange("p (h k) -> p h k", k=keys)
                diag = by_head[:, :, keys - P:keys]
                pe.matmul(diag, ident_b[:, :], mask_qk[:, :].unsqueeze(1).to_broadcast([P, len(heads), P]),
                          start=True, stop=False, skip_group_check=True)
                for m, h in enumerate(heads):
                    last = pe.matmul(by_head[:, m, :], q_stack[0:QK_ROWS, slot.par, h, i * P:(i + 1) * P],
                                     k_stack[0:QK_ROWS, slot.par, h, 0:keys], start=False, stop=True,
                                     skip_group_check=True)
                last.then_inc(s1_full, 1)

            def place(h):
                return 2 * (h % (HEADS // 2)) + h // (HEADS // 2)

            def group_heads(g):
                return [8 * (g // 2) + 2 * j + g % 2 for j in range(4)]

            def exp_scores(slot, n):
                g, part = divmod(n, 3)
                par = 1 - slot.par
                if n == 0:
                    wait(pe, max_stacked, slot, lambda t: 16 * t)
                    if slot.k is None:
                        pe.wait_ge(pads_set, 4)
                wait(pe, probs_ready, slot, lambda t: S2_BANKS * (t - 1) + n - 1)
                heads = group_heads(g)[2 * part:2 * part + 2] if part < 2 else group_heads(g)
                i, queries = (0, S) if part < 2 else (1, P)
                by_head = s2[:, n % 2, :].rearrange("p (h q) -> p h q", q=queries)
                pe.matmul(by_head[:, :, 0:P], ident_b[:, :], mask_kq[:, :].unsqueeze(1).to_broadcast([P, len(heads), P]),
                          start=True, stop=False, skip_group_check=True)
                for m, h in enumerate(heads):
                    last = pe.matmul(by_head[:, m, :], k_stack[0:S2_ROWS, par, place(h), i * P:(i + 1) * P],
                                     q_stack[0:S2_ROWS, par, place(h), S - queries:S], start=False, stop=True,
                                     skip_group_check=True)
                last.then_inc(s2_full, 1)

            def times_v(slot, g):
                half, which = divmod(g, 2)
                par = 1 - slot.par
                wait(pe, probs_ready, slot, lambda t: S2_BANKS * (t - 1) + 3 * (g + 1))
                if which == 0:
                    wait(pe, attn_ready, slot, lambda t: 2 * (t - 1) - 1 + half)
                for i, queries in ((0, S), (1, P)):
                    for j, h in enumerate(group_heads(g)):
                        b = (3 * g + (j // 2 if i == 0 else 2)) % PROB_RING
                        m = j % 2 if i == 0 else j
                        lhs = v_pad[:, par, i, h // 2, 2 * which:2 * which + 2, :].rearrange("p a r -> p (a r)")
                        last = pe.matmul(pv[32 * j:32 * (j + 1), half, which, S - queries:S], lhs,
                                         probs[:, b, m * queries:(m + 1) * queries],
                                         start=(which == 0 and i == 0), stop=(which == 1 and i == 1),
                                         skip_group_check=True)
                last.then_inc(pv_done, 1)

            def slot_pe(now):
                for name, n, slot in now.steps(PE_ORDER):
                    if name == "S1":
                        if slot.front:
                            max_scores(slot, n)
                    elif name == "S2":
                        if slot.middle:
                            exp_scores(slot, n)
                    elif name == "PV":
                        if slot.middle:
                            times_v(slot, n)
                    elif slot.has(name):
                        job_matmuls(slot, name)

            all_slots(pe, slot_pe)

            pe.wait_ge(stage_emptied[1], job_number(1))
            pe.wait_ge(c_ready, IMAGES + 1)
            by_token(1, whole_terms(c2, UX))


def _lay_out(inputs):
    a = {k: np.asarray(v) for k, v in inputs.items()}

    def tiles(w):
        return w.reshape(KT, P, D).transpose(1, 0, 2)

    def by_row_of_head(w):
        return w.reshape(D, 2, HEADS // 2, DH).transpose(0, 1, 3, 2).reshape(D, D)

    mats = [by_row_of_head(a["L0_attn_Wq"].T), by_row_of_head(a["L0_attn_Wk"].T), a["L0_attn_Wv"].T]
    mats += [a["L0_ffn_" + n].T for n in ("wf", "wi", "wc", "wo")] + [a["L0_attn_Wo"].T]
    mats += [a["L0_ffn_" + n].T for n in ("uf", "ui", "uc", "uo")]
    weights = np.stack([tiles(m) for m in mats], axis=1)

    vhd = [1, 0, 2]
    parts = []
    for lv, name in ((1, "Wd3"), (2, "Wd2"), (3, "Wd1")):
        rows, cols = (S >> lv) // 32, (D >> lv) // 2
        w = a["L0_tok_" + name].reshape(3, 32, rows, 2, cols, 3)[vhd][..., vhd]
        parts.append(w.transpose(1, 3, 5, 0, 2, 4).reshape(64, 9 * BAND[lv - 1]))
    parts.append(a["L0_tok_Wa"].reshape(32, 1, 2, 16).transpose(0, 2, 1, 3).reshape(64, BAND[2]))
    tok_w = np.concatenate(parts, axis=1)
    tok_w = np.concatenate([tok_w, tok_w], axis=0)
    tok_b = np.concatenate([a["L0_tok_ba"]] + [a["L0_tok_" + n][vhd] for n in ("bd1", "bd2", "bd3")])

    x = a["x"].reshape(PAIRS, 2, S // BR, BR, 2, BC).transpose(0, 1, 2, 4, 3, 5).reshape(PAIRS, P, XW)
    col_b = np.stack([a["L0_ffn_" + n].reshape(KT, P).T for n in ("bf", "bi", "bc", "in_c")], axis=1)
    high = (np.arange(P) // DH % 2).astype(np.float32)
    halves = np.stack([1 - high, high], axis=1)
    arrays = {"x_in": x, "weights_in": weights, "tok_w_in": tok_w, "tok_b_in": tok_b, "col_b_in": col_b,
              "bo_in": a["L0_ffn_bo"], "halves_in": halves}
    return {k: np.ascontiguousarray(v) for k, v in arrays.items()}


def kernel(**inputs):
    import concourse.bacc as bacc
    from concourse.bass_utils import run_bass_kernel_spmd

    nc = bacc.Bacc("TRN2", target_bir_lowering=False, num_devices=1)
    arrays = _lay_out(inputs)
    args = [nc.dram_tensor(k, v.shape, mybir.dt.from_np(v.dtype), kind="ExternalInput").ap() for k, v in arrays.items()]
    out = nc.dram_tensor("out", (IMAGES, S, D), F32, kind="ExternalOutput").ap()
    scratch = nc.dram_tensor("scratch", (PAIRS, P, XW), F32, kind="Internal").ap()
    spill = nc.dram_tensor("spill", (IMAGES, P, IMG), F32, kind="Internal").ap()
    build(nc, *args, out, scratch, spill)
    result = run_bass_kernel_spmd(nc, [arrays], core_ids=[0])
    return result.results[0]["out"]
```

```python
from contextlib import ExitStack

import numpy as np

import concourse.bass as bass
from concourse import mybir

F32 = mybir.dt.float32
F32R = mybir.dt.float32r
BF16 = mybir.dt.bfloat16
ALU = mybir.AluOpType
ACT = mybir.ActivationFunctionType
AX_X = mybir.AxisListType.X

P = 128
IMAGES = 16
S = 256
D = 256
HEADS = 16
DH = D // HEADS
TILES = S // P
KT = D // P
IMG = TILES * D
EPS = 1e-5
SCALE = DH ** -0.5
MASKED = -1e30
LOWEST = -3e38

Q_BLOCKS = (0, 0, 1, 1, 0, 2)
K_BLOCKS = (0, 1, 0, 1, 2, 0)
QK_ROWS = len(Q_BLOCKS) * DH
MAX_PARTS = 2
S2_ROWS = QK_ROWS + MAX_PARTS

PAIRS = IMAGES // 2
BR, BC = 8, 128
XW = BR * BC
LEVELS = 3
BAND = [XW >> (2 * lv) for lv in range(1, LEVELS + 1)]
TOK_FWD, TOK_SCALE, TOK_INV = 12, 4, 12
TOK_STEPS = TOK_FWD + TOK_SCALE + TOK_INV
GROUPS = 4
LOGITS = 3 * GROUPS
W_OFF = {1: 0, 2: 9 * BAND[0], 3: 9 * (BAND[0] + BAND[1])}
W_A = 9 * sum(BAND)
W_ALL = W_A + BAND[2]

SPLIT = WQ, WK, WV, WF, WI, WC, WX, UF, UI, UC = range(10)
WHOLE = WO, UX = range(2)
RING = 8

S1_BANKS = 12
S1_RING = 2
S2_BANKS = 12
PROB_RING = 6
PV_GROUPS = 4

PE_ORDER = """XT1 PV_3' S1_10' S1_11' Q MT K S2_0 S2_1 WO S2_2 S2_3 V S2_4 PV_0 S2_5 S2_6 SUM XT2 PV_1 S2_7 S1_0 S1_1
    S2_8 F S1_2 PV_2 S1_3 S2_9 I S1_4 G S1_5 S2_10 S1_6 X S1_7 S2_11 S1_8 S1_9""".split()
ACT_ORDER = """CHI' XT1 HALF_1' Q MT K Q2 E_0 E_1 K2 E_2 E_3 V E_4 LN2 E_5 EXP3 XT2 E_6 HALF_0 E_7 E_8 E_9 F I G LN1
    E_10 X E_11""".split()
DVE_ORDER = """XT1 M_10' M_11' NEG HALF_1' Q DOTS_0 DOTS_1 Q3 DOTS_2 K WO STATS2 DOTS_3 K3 SHIFT2 DOTS_4 LOGITS XT2 M_0
    M_1 HALF_0 M_2 M_3 C_0 SOFTMAX STATS1 M_4 M_5 SHIFT1 C_1 M_6 M_7 M_8 M_9 CLO""".split()
POOL_ORDER = """FWD_0 FWD_1 BWD_0 FWD_2 FWD_3 BWD_1 BWD_2 FWD_4 FWD_5 FWD_6 FWD_7 FWD_8 FWD_9 BWD_3 FWD_10 BWD_4 BWD_5
    BWD_6 FWD_11 BWD_7 BWD_8 BWD_9 BWD_10 BWD_11 BWD_12 BWD_13 BWD_14 BWD_15 RSTD2 RSTD1""".split()
SP_ORDER = """MT P_0 P_1 P_2 SPILL PAIR""".split()
JOB_BANK = {"XT1": 2, "Q": 1, "K": 2, "WO": 0, "V": 1, "SUM": 2, "XT2": 0, "F": 1, "I": 2, "G": 0, "X": 2}
LATE = "'"
FRONT, BACK = ("XT1", "Q", "K", "V"), ("WO", "XT2", "F", "I", "G", "X")

FIRST_LOOPED, LOOPS = 4, 5
SLOTS = IMAGES + 2


def runs(t, job):
    if job == "SUM":
        return t >= 0 and t % 2 == 0 and t // 2 + 1 < PAIRS
    if job == "MT":
        return 1 <= t <= IMAGES
    return 0 <= t < IMAGES if job in FRONT else 2 <= t < SLOTS


def job_number(bank, of_slot=None, of_job=None):
    n = 1 if bank == JOB_BANK["SUM"] else 0
    for t in range(SLOTS + 1):
        for step in PE_ORDER:
            job, at = step.rstrip(LATE), t - step.endswith(LATE)
            if job in JOB_BANK and JOB_BANK[job] == bank:
                if (at, job) == (of_slot, of_job):
                    return n
                n += runs(at, job)
    return n


def jobs_before(t, job):
    return job_number(JOB_BANK[job], t, job)


class Slot:

    def __init__(self, t, k=None):
        self.t, self.k = t, k
        self.par = t % 2
        looped = k is not None
        self.front = looped or 0 <= t < IMAGES
        self.middle = looped or 1 <= t <= IMAGES
        self.back = looped or 2 <= t < SLOTS
        self.pair = looped or t >= 0 and t // 2 + 1 < PAIRS
        self.next_front = looped or 0 <= t < IMAGES - 1

    def has(self, job):
        if job == "SUM":
            return self.pair and self.par == 0
        if job == "MT":
            return self.middle
        return self.front if job in FRONT else self.back

    def steps(self, order):
        before = Slot(self.t - 1, self.k)
        for step in order:
            name, _, n = step.rstrip(LATE).partition("_")
            yield name, int(n or 0), before if step.endswith(LATE) else self

    def at(self, count):
        if self.k is None:
            return count(self.t)
        return self.k * (count(self.t + 2) - count(self.t)) + count(self.t)


def wait(eng, sem, slot, count):
    if slot.k is None and count(slot.t) <= 0:
        return
    assert count(slot.t) > 0
    eng.wait_ge(sem, slot.at(count))


def all_slots(eng, body):
    for t in range(FIRST_LOOPED):
        body(Slot(t))
    with eng.Fori(0, LOOPS) as k:
        for s in range(2):
            body(Slot(FIRST_LOOPED + s, k))
    for t in range(FIRST_LOOPED + 2 * LOOPS, SLOTS + 1):
        body(Slot(t))


def build(nc, x, weights, tok_w, tok_b, col_b, bo, halves, out, scratch, spill):
    ctx = ExitStack()
    with ctx:
        def sb(name, shape, dt=F32):
            return ctx.enter_context(nc.sbuf_tensor(name, shape, dt))

        def ps(name, shape):
            return ctx.enter_context(nc.psum_tensor(name, shape, F32))

        def sem(name):
            return ctx.enter_context(nc.semaphore(name))

        hidden = sb("hidden", [P, RING * IMG])
        xo = sb("xo", [P, IMAGES * IMG])
        w_hi = sb("w_hi", [P, len(SPLIT), KT, D], F32R)
        w_lo = sb("w_lo", [P, len(SPLIT), KT, D], F32R)
        w_all = sb("w_all", [P, len(WHOLE), KT, D])
        w_raw = xo[:, (IMAGES - len(SPLIT)) * IMG:].rearrange("p (w k c) -> p w k c", w=len(SPLIT), k=KT)
        q_stack = sb("q_stack", [P, 2, HEADS, S], BF16)
        k_stack = sb("k_stack", [P, 2, HEADS, S], BF16)
        early = q_stack[:, :, :, :].rearrange("p a h t -> p (a h t)").bitcast(F32)
        q_parts = sb("q_parts", [P, 3, 2, S], BF16)
        k_parts = sb("k_parts", [P, 3, 2, S], BF16)
        q_rest = sb("q_rest", [P, 2 * S])
        k_rest = sb("k_rest", [P, 2 * S])
        v_pad = sb("v_pad", [P, 2, TILES, HEADS // 2, 4, DH])
        xn = sb("xn", [P, TILES, D])
        xt = [sb("xt_hi", [P, KT, S], F32R), sb("xt_lo", [P, KT, S], F32R)]
        c_split = [sb("c_hi", [P, KT, S], F32R), sb("c_lo", [P, KT, S], F32R)]
        probs = sb("probs", [P, PROB_RING, 512])
        first_v = sb("first_v", [P, S])
        second_sum = sb("second_sum", [P, S])
        row_sum = sb("row_sum", [P, S])
        row_inv = sb("row_inv", [P, S])
        side = sb("side", [P, 2])
        low16, high16 = side[:, 0:1], side[:, 1:2]
        attn_t = sb("attn_t", [P, 2, S])
        gate = sb("gate", [P, 3, 2, S])
        c2 = sb("c2", [P, KT, S])
        row_max = sb("row_max", [P, TILES, HEADS])
        neg_max_parts = sb("neg_max_parts", [P, TILES, MAX_PARTS, HEADS], BF16)
        max_rows = sb("max_rows", [MAX_PARTS * HEADS, S], BF16)
        bn1 = sb("bn1", [P, TILES, 6])
        bn2 = sb("bn2", [P, TILES, 6])
        mv1 = sb("mv1", [P, TILES, 2])
        mv2 = sb("mv2", [P, TILES, 2])
        ln1 = sb("ln1", [P, 3, TILES])
        ln2 = sb("ln2", [P, 3, TILES])
        tok_x = sb("tok_x", [P, XW])
        tok_t = sb("tok_t", [P, XW])
        tok_c = {lv: sb(f"tok_c{lv}", [P, 4 * BAND[lv - 1]]) for lv in (1, 2, 3)}
        tok_weights = sb("tok_weights", [P, W_ALL])
        dots = sb("dots", [P, LOGITS])
        logit = sb("logit", [P, LOGITS])
        logit_b = sb("logit_b", [P, LOGITS])
        logit_s = sb("logit_s", [P, LOGITS])
        band_s = sb("band_s", [P, LOGITS])
        tok_max = sb("tok_max", [P, GROUPS])
        tok_sum = sb("tok_sum", [P, GROUPS])
        tok_exp = sb("tok_exp", [P, LOGITS])
        band_w = sb("band_w", [P, LOGITS])
        half_col = sb("half_col", [P, 4, KT])
        gate_b = sb("gate_b", [P, 3, KT])
        bo_row = sb("bo_row", [P, D])
        cu = xn
        ident = sb("ident", [P, P])
        ident_b = sb("ident_b", [P, P], BF16)
        mask_qk = sb("mask_qk", [P, P], BF16)
        mask_kq = sb("mask_kq", [P, P], BF16)
        same_image = sb("same_image", [P, P])
        neg_half = sb("neg_half", [P, TILES])
        eps = sb("eps", [P, TILES])
        spare = sb("spare", [P, 1])
        max_spare = sb("max_spare", [P, 4])

        stage = ps("stage", [P, 3, 512])
        s1 = ps("s1", [P, S1_RING, 512])
        s2 = ps("s2", [P, 2, 512])
        pv = ps("pv", [P, 2, S])

        mt_rows = s2[0:MAX_PARTS * HEADS, 0, :].bitcast(BF16)

        mt_full, mt_emptied = sem("mt_full"), sem("mt_emptied")
        consts_set = sem("consts_set")
        pool_set = sem("pool_set")
        pads_set = sem("pads_set")
        dve_set = sem("dve_set")
        tok_in = sem("tok_in")
        tokw_in = sem("tokw_in")
        small_in = sem("small_in")
        qkv_in = sem("qkv_in")
        rest_in = sem("rest_in")
        ffn_in = sem("ffn_in")
        w_hi_ready, w_lo_ready = sem("w_hi_ready"), sem("w_lo_ready")
        xt_hi_ready = [sem("xt1_hi_ready"), sem("xt2_hi_ready")]
        parts_ready, pair_ready, sum_ready, turned_ready = (sem(n) for n in ("parts_ready", "pair_ready", "sum_ready",
                                                                             "turned_ready"))
        spilled, reloaded = sem("spilled"), [sem("reloaded_0_to_3"), sem("reloaded_4_to_7")]
        x_in = tok_in
        u_scaled = sem("u_scaled")
        c_hi_ready, c_lo_ready = sem("c_hi_ready"), sem("c_lo_ready")
        tok_step = sem("tok_step")
        dots_done = sem("dots_done")
        tok_small = sem("tok_small")
        tok_exp_done = sem("tok_exp_done")
        rec_out = sem("rec_out")
        hidden_in = [sem("hidden_in_even"), sem("hidden_in_odd")]
        stage_full = [sem("stage_full0"), sem("stage_full1"), sem("stage_full2")]
        stage_emptied = [sem("stage_emptied0"), sem("stage_emptied1"), sem("stage_emptied2")]
        q1_ready, q2_ready, q3_ready = sem("q1_ready"), sem("q2_ready"), sem("q3_ready")
        k1_ready, k2_ready, k3_ready = sem("k1_ready"), sem("k2_ready"), sem("k3_ready")
        q_stacked = sem("q_stacked")
        k_stacked = sem("k_stacked")
        max_stacked = sem("max_stacked")
        s1_full, s1_emptied = sem("s1_full"), sem("s1_emptied")
        s2_full, probs_ready = sem("s2_full"), sem("probs_ready")
        max_part1, max_parts_ready = sem("max_part1"), sem("max_parts_ready")
        pv_done, inv_ready, attn_ready = sem("pv_done"), sem("inv_ready"), sem("attn_ready")
        bn_done = [sem("bn1_done"), sem("bn2_done")]
        mv_done = [sem("mv1_done"), sem("mv2_done")]
        eps_done = [sem("eps1_done"), sem("eps2_done")]
        rstd_done = [sem("rstd1_done"), sem("rstd2_done")]
        shift_done = [sem("shift1_done"), sem("shift2_done")]
        xn_ready = [sem("xn1_ready"), sem("xn2_ready")]
        c_half = sem("c_half")
        c_ready = sem("c_ready")
        cu_ready = sem("cu_ready")
        pre_ready, tanh_ready = sem("pre_ready"), sem("tanh_ready")
        out_even, out_odd = sem("out_even"), sem("out_odd")
        stored = sem("stored")

        block = ctx.enter_context(nc.Block())

        def full(eng, slot, job):
            wait(eng, stage_full[JOB_BANK[job]], slot, lambda t: jobs_before(t, job) + 1)

        def emptied(eng, slot, job):
            wait(eng, stage_emptied[JOB_BANK[job]], slot, lambda t: jobs_before(t, job) + 1)

        def bank(job):
            return stage[:, JOB_BANK[job], :]

        def residual(slot, back):
            return hidden[:, bass.ds(slot.at(lambda t: t - back) % RING * IMG, IMG)]

        def tok_wait(eng, slot, n):
            wait(eng, tok_step, slot, lambda t: TOK_STEPS * (t // 2 + 1) + n)

        def tok_forward(eng, slot, pieces=range(TOK_FWD)):
            for piece in pieces:
                lv, part = piece // 4 + 1, piece % 4
                src, n = (tok_x, tok_c[1], tok_c[2])[lv - 1], XW >> 2 * (lv - 1)
                h, c = n // 2, BC >> lv
                op = (ALU.add, ALU.subtract)[part % 2]
                at = slice(part % 2 * h, (part % 2 + 1) * h)
                if part < 2:
                    even = src[:, 0:n].rearrange("p (n two) -> p two n", two=2)
                    if lv > 1:
                        tok_wait(eng, slot, piece - part)
                    eng.tensor_tensor(tok_t[:, at], even[:, 0], even[:, 1], op).then_inc(tok_step, 1)
                else:
                    rows = tok_t[:, 0:n].rearrange("p (m two c) -> p two m c", two=2, c=c)
                    tok_wait(eng, slot, piece - part + 2)
                    eng.tensor_tensor(tok_c[lv][:, at].rearrange("p (m c) -> p m c", c=c), rows[:, 0], rows[:, 1],
                                      op).then_inc(tok_step, 1)

        def tok_backward(eng, slot, pieces=range(TOK_SCALE + TOK_INV)):
            for piece in pieces:
                if piece == 0:
                    n3 = BAND[2]
                    eng.tensor_tensor(tok_c[3][:, 0:n3], tok_c[3][:, 0:n3], band_w[:, 0:1].to_broadcast([P, n3]),
                                      ALU.mult).then_inc(tok_step, 1)
                elif piece < TOK_SCALE:
                    lv = TOK_SCALE - piece
                    n, g = BAND[lv - 1], GROUPS - lv
                    bands = tok_c[lv][:, n:4 * n].rearrange("p (b n) -> p b n", b=3)
                    wts = band_w[:, 3 * g:3 * g + 3].unsqueeze(2).to_broadcast([P, 3, n])
                    eng.tensor_tensor(bands, bands, wts, ALU.mult).then_inc(tok_step, 1)
                else:
                    lv, part = LEVELS - piece // 4 + 1, piece % 4
                    n = 4 * BAND[lv - 1]
                    h, c = n // 2, BC >> lv
                    op = (ALU.add, ALU.subtract)[part % 2]
                    if part < 2:
                        rows = tok_t[:, 0:n].rearrange("p (m two c) -> p two m c", two=2, c=c)
                        av = tok_c[lv][:, 0:h].rearrange("p (m c) -> p m c", c=c)
                        hd = tok_c[lv][:, h:n].rearrange("p (m c) -> p m c", c=c)
                        tok_wait(eng, slot, TOK_FWD + piece - part)
                        eng.tensor_tensor(rows[:, part], av, hd, op).then_inc(tok_step, 1)
                    else:
                        dst = tok_x if lv == 1 else tok_c[lv - 1]
                        cols = dst[:, 0:n].rearrange("p (n two) -> p two n", two=2)
                        tok_wait(eng, slot, TOK_FWD + piece - part + 2)
                        eng.tensor_tensor(cols[:, part - 2], tok_t[:, 0:h], tok_t[:, h:n], op).then_inc(tok_step, 1)

        DOTS = 10
        DOT_PIECES = ((0, 4), (4, 7), (7, 8), (8, 9), (9, 10))
        FIRST_PAIR = Slot(-2)

        def tok_dots(eng, slot, piece):
            if piece == 0:
                tok_wait(eng, slot, TOK_FWD)
            columns = [(0, 3, 0, BAND[2], W_A)]
            for lv in (3, 2, 1):
                n, g = 3 * BAND[lv - 1], GROUPS - lv
                columns += [(3 * g + j, lv, n // 3, n, W_OFF[lv] + j * n) for j in range(3)]
            for i in range(*DOT_PIECES[piece]):
                col, lv, first, n, off = columns[i]
                products = (tok_t, tok_x)[i % 2]
                if i >= 2:
                    wait(eng, dots_done, slot, lambda t: DOTS * (t // 2 + 1) + i - 1)
                eng.tensor_tensor_reduce(products[:, 0:n], tok_c[lv][:, first:first + n], tok_weights[:, off:off + n],
                                         1.0, 0.0, ALU.mult, ALU.add, dots[:, col:col + 1]).then_inc(dots_done, 1)

        SMALL = 7

        def small_wait(eng, slot, n):
            wait(eng, tok_small, slot, lambda t: SMALL * (t // 2 + 1) + n)

        def tok_logits(eng, slot):
            l3 = logit[:, :].rearrange("p (g j) -> p g j", j=3)
            if slot is FIRST_PAIR:
                eng.wait_ge(stage_full[JOB_BANK["SUM"]], 1)
            else:
                full(eng, slot, "SUM")
            eng.tensor_tensor(logit[:, :], bank("SUM")[:, 0:LOGITS], logit_s[:, :], ALU.mult)\
               .then_inc(stage_emptied[JOB_BANK["SUM"]], 1)
            if slot is FIRST_PAIR:
                eng.wait_ge(stage_emptied[JOB_BANK["SUM"]], 1)
            else:
                emptied(eng, slot, "SUM")
            eng.tensor_tensor(logit[:, :], logit[:, :], logit_b[:, :], ALU.add).then_inc(tok_small, 1)
            small_wait(eng, slot, 1)
            eng.tensor_reduce(tok_max[:, :], l3, AX_X, ALU.max).then_inc(tok_small, 1)
            small_wait(eng, slot, 2)
            eng.tensor_tensor(l3, l3, tok_max[:, :].unsqueeze(2).to_broadcast([P, GROUPS, 3]), ALU.subtract)\
               .then_inc(tok_small, 1)

        def tok_exps(eng, slot):
            small_wait(eng, slot, 3)
            eng.activation(tok_exp[:, :], logit[:, :], ACT.Exp).then_inc(tok_exp_done, 1)

        def tok_softmax(eng, slot):
            e3 = tok_exp[:, :].rearrange("p (g j) -> p g j", j=3)
            wait(eng, tok_exp_done, slot, lambda t: t // 2 + 2)
            eng.tensor_reduce(tok_sum[:, :], e3, AX_X, ALU.add).then_inc(tok_small, 1)
            small_wait(eng, slot, 4)
            eng.reciprocal(tok_max[:, :], tok_sum[:, :]).then_inc(tok_small, 1)
            small_wait(eng, slot, 5)
            eng.tensor_tensor(e3, e3, tok_max[:, :].unsqueeze(2).to_broadcast([P, GROUPS, 3]), ALU.mult)\
               .then_inc(tok_small, 1)
            small_wait(eng, slot, 6)
            eng.tensor_tensor(band_w[:, :], tok_exp[:, :], band_s[:, :], ALU.mult).then_inc(tok_small, 1)

        def tok_sum_matmul(eng):
            eng.matmul(bank("SUM")[:, 0:LOGITS], same_image[:, :], dots[:, :], start=True, stop=True)\
               .then_inc(stage_full[JOB_BANK["SUM"]], 1)

        LN = [(bn1, mv1, ln1), (bn2, mv2, ln2)]
        LN_COUNT = [lambda t: t + 2, lambda t: t - 1]

        def ln_stats(eng, slot, which):
            bn, mv, _ = LN[which]
            src = residual(slot, -1 if which == 0 else 2).rearrange("p (i c) -> p i c", i=TILES)
            eng.memset(spare[:, :], 0.0)
            for i in range(TILES):
                last = eng.bn_stats(bn[:, i, :], src[:, i, :])
            last.then_inc(bn_done[which], 1)
            wait(eng, bn_done[which], slot, LN_COUNT[which])
            eng.memset(spare[:, :], 0.0)
            for i in range(TILES):
                last = eng.bn_aggr(mv[:, i, :], bn[:, i, :])
            last.then_inc(mv_done[which], 1)

        def ln_rstd(eng, slot, which):
            _, mv, ln = LN[which]
            wait(eng, mv_done[which], slot, LN_COUNT[which])
            eng.tensor_tensor(ln[:, 0, :], mv[:, :, 1], eps[:, :], ALU.add).then_inc(eps_done[which], 1)
            wait(eng, eps_done[which], slot, LN_COUNT[which])
            eng.tensor_tensor(ln[:, 1, :], ln[:, 0, :], neg_half[:, :], ALU.pow).then_inc(rstd_done[which], 1)

        def ln_shift(eng, slot, which):
            _, mv, ln = LN[which]
            wait(eng, rstd_done[which], slot, LN_COUNT[which])
            eng.scalar_tensor_tensor(out=ln[:, 2, :], in0=mv[:, :, 0], scalar=-1.0, in1=ln[:, 1, :],
                                     op0=ALU.mult, op1=ALU.mult).then_inc(shift_done[which], 1)

        def ln_apply(eng, slot, which):
            _, _, ln = LN[which]
            src = residual(slot, -1 if which == 0 else 2).rearrange("p (i c) -> p i c", i=TILES)
            wait(eng, shift_done[which], slot, LN_COUNT[which])
            for i in range(TILES):
                last = eng.activation(xn[:, i, :], src[:, i, :], ACT.Identity, scale=ln[:, 1, i:i + 1],
                                      bias=ln[:, 2, i:i + 1])
            last.then_inc(xn_ready[which], 1)

        START = Slot(1)
        BEFORE_FIRST = Slot(-1)

        def store_pair(sp, p_value):
            sp.dma_start(scratch[bass.ds(p_value, 1)].rearrange("o p x -> (o p) x"), tok_x[:, :]).then_inc(rec_out, 16)

        def load_hidden(sp, p_value, first_image, of_pair=range(2)):
            pair = scratch[bass.ds(p_value, 1)].rearrange("o (i b ch) (r c) -> (o i) b r ch c", i=2, ch=2, c=BC)
            for i in of_pair:
                for tile in range(TILES):
                    blocks = P // BR
                    off = (first_image % RING + i) * IMG + tile * D
                    for ch in range(2):
                        sp.dma_start(hidden[:, bass.ds(off + ch * BC, BC)],
                                     pair[i, tile * blocks:(tile + 1) * blocks, :, ch, :]).then_inc(hidden_in[i], 16)

        HIDDEN_DMAS = TILES * 2 * 16

        @block.sync
        def _(sp):
            sp.dma_start(tok_x[:, :], x[0]).then_inc(tok_in, 16)
            sp.dma_start(tok_weights[:, :], tok_w).then_inc(tokw_in, 16)
            sp.dma_start(logit_b[:, 0:1], tok_b[0:1].partition_broadcast(P)).then_inc(small_in, 16)
            sp.dma_start(logit_b[:, 3:LOGITS], tok_b[1:10].partition_broadcast(P)).then_inc(small_in, 16)
            sp.dma_start(half_col[:, :, :], col_b).then_inc(small_in, 16)
            sp.dma_start(side[:, :], halves).then_inc(small_in, 16)
            sp.dma_start(bo_row[:, :], bo.partition_broadcast(P)).then_inc(small_in, 16)
            sp.dma_start(w_raw[:, WQ:WF], weights[:, WQ:WF]).then_inc(qkv_in, 16)
            sp.dma_start(w_raw[:, WF:], weights[:, WF:len(SPLIT)]).then_inc(ffn_in, 16)
            sp.dma_start(w_all[:, :, :, :], weights[:, len(SPLIT):]).then_inc(rest_in, 16)
            sp.wait_ge(tok_step, TOK_STEPS)
            store_pair(sp, 0)
            sp.wait_ge(rec_out, 16)
            load_hidden(sp, 0, 0, [0])
            sp.dma_start(tok_x[:, :], x[1]).then_inc(tok_in, 16)
            load_hidden(sp, 0, 0, [1])

            def slot_dmas(now):
                slot = now
                if slot.pair and slot.par == 0 and slot.t > 0:
                    p_value = slot.at(lambda t: t // 2 + 1)
                    pixels = x[p_value] if slot.k is None else x[bass.ds(p_value, 1)].rearrange("o p x -> (o p) x")
                    sp.dma_start(tok_x[:, :], pixels).then_inc(tok_in, 16)
                for name, n, slot in now.steps(SP_ORDER):
                    if name == "MT" and slot.middle:
                        wait(sp, mt_emptied, slot, lambda t: t)
                        sp.dma_start(q_stack[QK_ROWS:S2_ROWS, 1 - slot.par].rearrange("r h t -> r (h t)"),
                                     max_rows[:, :]).then_inc(max_stacked, 16)
                    if name == "P" and slot.front:
                        part = n
                        for ready, sem_, parts, stack, blocks in (
                                ((q1_ready, q2_ready, q3_ready)[part], q_stacked, q_parts, q_stack, Q_BLOCKS),
                                ((k1_ready, k2_ready, k3_ready)[part], k_stacked, k_parts, k_stack, K_BLOCKS)):
                            wait(sp, ready, slot, lambda t: t + 1)
                            for b in range(len(blocks)):
                                if blocks[b] == part:
                                    sp.dma_start(stack[DH * b:DH * (b + 1), slot.par].rearrange("r h t -> r (h t)"),
                                                 parts[:, part].rearrange("p m t -> p (m t)")).then_inc(sem_, 16)
                    if name == "SPILL" and slot.back and (slot.k is not None or slot.t - 2 < RING):
                        emptied(sp, slot, "WO")
                        sp.dma_start(spill[bass.ds(slot.at(lambda t: t - 2), 1)].rearrange("o p x -> (o p) x"),
                                     residual(slot, 2)).then_inc(spilled, 16)
                    if name == "PAIR" and slot.pair and slot.par == 1:
                        if slot.k is not None:
                            wait(sp, spilled, slot, lambda t: 16 * (t - 1))
                        tok_wait(sp, slot, TOK_STEPS)
                        p_value = slot.at(lambda t: t // 2 + 1)
                        store_pair(sp, p_value)
                        wait(sp, rec_out, slot, lambda t: 16 * (t // 2 + 2))
                        load_hidden(sp, p_value, slot.at(lambda t: t + 1))

            all_slots(sp, slot_dmas)

            sp.wait_ge(spilled, 16 * RING)
            for par in range(2):
                sp.wait_ge(s2_full, S2_BANKS * (IMAGES - 1 + par))
                sp.dma_start(early[:, par * RING // 2 * IMG:(par + 1) * RING // 2 * IMG].rearrange("p (o x) -> p o x", x=IMG),
                             spill[par * RING // 2:(par + 1) * RING // 2].rearrange("o p x -> p o x"))\
                  .then_inc(reloaded[par], 16)

            with sp.Fori(0, IMAGES // 2) as k:
                for s, ready in ((0, out_even), (1, out_odd)):
                    sp.wait_ge(ready, k + 1)
                    sp.dma_start(out[bass.ds((2 * k + s + RING) % IMAGES, 1)].rearrange("o (i p) c -> p (o i) c", p=P),
                                 xo[:, bass.ds((2 * k + s + RING) % IMAGES * IMG, IMG)]
                                 .rearrange("p (i c) -> p i c", i=TILES)).then_inc(stored, 16)
            sp.wait_ge(stored, 16 * IMAGES)

        @block.gpsimd
        def _(pool):
            pool.memset(ident[:, :], 0.0).then_inc(pool_set, 1)
            pool.memset(ident_b[:, :], 0.0).then_inc(pool_set, 1)
            pool.memset(mask_qk[:, :], 0.0).then_inc(pool_set, 1)
            pool.memset(mask_kq[:, :], 0.0).then_inc(pool_set, 1)
            pool.wait_ge(pool_set, 4)
            for m in (ident, ident_b):
                pool.affine_select(out=m[:, :], in_=m[:, :], compare_op=ALU.not_equal, fill=1.0, base=0,
                                   pattern=[[-1, P]], channel_multiplier=1).then_inc(consts_set, 1)
            pool.affine_select(out=mask_qk[:, :], in_=mask_qk[:, :], compare_op=ALU.is_ge, fill=MASKED, base=0,
                               pattern=[[-1, P]], channel_multiplier=1).then_inc(consts_set, 1)
            pool.affine_select(out=mask_kq[:, :], in_=mask_kq[:, :], compare_op=ALU.is_ge, fill=MASKED, base=0,
                               pattern=[[1, P]], channel_multiplier=-1).then_inc(consts_set, 1)
            for par in range(2):
                pool.memset(v_pad[:, par], 1.0).then_inc(pads_set, 1)
            pool.wait_ge(consts_set, 7)
            pool.wait_ge(pads_set, 2)
            for par in range(2):
                pool.memset(k_stack[QK_ROWS:S2_ROWS, par, :, :], 1.0).then_inc(pads_set, 1)
            pool.wait_ge(pads_set, 4)
            for first, end, arrived in ((WQ, WF, qkv_in), (WF, len(SPLIT), ffn_in)):
                pool.wait_ge(arrived, 16)
                for w in range(first, end):
                    pool.wait_ge(w_hi_ready, w + 1)
                    pool.tensor_tensor(w_lo[:, w], w_raw[:, w], w_hi[:, w], ALU.subtract).then_inc(w_lo_ready, 1)
            ln_rstd(pool, BEFORE_FIRST, 0)

            def slot_pool(now):
                for name, n, slot in now.steps(POOL_ORDER):
                    if name == "FWD" and slot.pair and slot.par == 0:
                        if n == 0:
                            wait(pool, tok_in, slot, lambda t: 16 * (t // 2 + 2))
                        tok_forward(pool, slot, [n])
                    elif name == "BWD" and slot.pair and slot.par == 1:
                        if n == 0:
                            small_wait(pool, slot, SMALL)
                        tok_backward(pool, slot, [n])
                    elif name == "RSTD2" and slot.back:
                        ln_rstd(pool, slot, 1)
                    elif name == "RSTD1" and slot.next_front:
                        ln_rstd(pool, slot, 0)

            all_slots(pool, slot_pool)

            def finish_even(k, kept, first):
                xo_at = bass.ds((2 * k + RING) % IMAGES * IMG, IMG)
                pool.wait_ge(tanh_ready, 2 * k + 1)
                pool.tensor_tensor(xo[:, xo_at], xo[:, xo_at], kept[:, bass.ds((2 * k - first) * IMG, IMG)], ALU.add)\
                    .then_inc(out_even, 1)

            with pool.Fori(0, RING // 2) as k:
                finish_even(k, hidden, 0)
            for par in range(2):
                pool.wait_ge(reloaded[par], 16)
            with pool.Fori(RING // 2, IMAGES // 2) as k:
                finish_even(k, early, RING)

        @block.scalar
        def _(act):
            for first, end, arrived in ((WQ, WF, qkv_in), (WF, len(SPLIT), ffn_in)):
                act.wait_ge(arrived, 16)
                for w in range(first, end):
                    act.copy(w_hi[:, w], w_raw[:, w]).then_inc(w_hi_ready, 1)
                if first == WQ:
                    tok_exps(act, FIRST_PAIR)
            ln_apply(act, BEFORE_FIRST, 0)

            def split_state_hi(slot):
                wait(act, c_ready, slot, lambda t: t)
                act.activation(c_split[0][:, :, :], c2[:, :, :], ACT.Copy, scale=0.5).then_inc(c_hi_ready, 1)

            split_state_hi(START)

            def slot_act(now):
                for name, n, slot in now.steps(ACT_ORDER):
                    if name == "XT1" and slot.front:
                        full(act, slot, "XT1")
                        act.copy(xt[0][:, :, :], bank("XT1").rearrange("p (k t) -> p k t", k=KT))\
                           .then_inc(xt_hi_ready[0], 1)
                    elif name == "Q" and slot.front:
                        full(act, slot, "Q")
                        wait(act, q_stacked, slot, lambda t: 96 * t)
                        act.copy(q_parts[:, 0], bank("Q").rearrange("p (m t) -> p m t", m=2)).then_inc(q1_ready, 1)
                    elif name == "K" and slot.front:
                        full(act, slot, "K")
                        wait(act, k_stacked, slot, lambda t: 96 * t)
                        act.copy(k_parts[:, 0], bank("K").rearrange("p (m t) -> p m t", m=2)).then_inc(k1_ready, 1)
                    elif name == "Q2" and slot.front:
                        emptied(act, slot, "Q")
                        act.copy(q_parts[:, 1], q_rest[:, :].rearrange("p (m t) -> p m t", m=2)).then_inc(q2_ready, 1)
                    elif name == "K2" and slot.front:
                        emptied(act, slot, "K")
                        act.copy(k_parts[:, 1], k_rest[:, :].rearrange("p (m t) -> p m t", m=2)).then_inc(k2_ready, 1)
                    elif name == "V" and slot.front:
                        if slot.k is None and slot.t == 0:
                            act.wait_ge(pads_set, 4)
                        full(act, slot, "V")
                        src = bank("V").rearrange("p (i g s r) -> p i g s r", i=TILES, s=2, r=DH)
                        for i in range(TILES):
                            last = act.copy(v_pad[:, slot.par, i, :, 0:4:3, :], src[:, i])
                        last.then_inc(stage_emptied[JOB_BANK["V"]], 1)
                    elif name == "LN2" and slot.back:
                        ln_apply(act, slot, 1)
                    elif name == "XT2" and slot.back:
                        full(act, slot, "XT2")
                        act.copy(xt[0][:, :, :], bank("XT2").rearrange("p (k t) -> p k t", k=KT))\
                           .then_inc(xt_hi_ready[1], 1)
                    elif name in ("F", "I", "G") and slot.back:
                        g = "FIG".index(name)
                        full(act, slot, name)
                        wait(act, c_ready, slot, lambda t: t - 1)
                        for m in range(KT):
                            last = act.activation(gate[:, g, m, :], bank(name)[:, m * S:(m + 1) * S], ACT.Tanh,
                                                  scale=0.5 if name in "FI" else 1.0, bias=gate_b[:, g, m:m + 1])
                        last.then_inc(stage_emptied[JOB_BANK[name]], 1)
                    elif name == "X" and slot.back:
                        full(act, slot, "X")
                        act.copy(xo[:, bass.ds(slot.at(lambda t: (t - 2) * IMG), IMG)], bank("X"))\
                           .then_inc(stage_emptied[JOB_BANK["X"]], 1)
                    elif name == "MT" and slot.middle:
                        wait(act, mt_full, slot, lambda t: t)
                        wait(act, max_stacked, slot, lambda t: 16 * (t - 1))
                        act.copy(max_rows[:, :], mt_rows[:, 0:S]).then_inc(mt_emptied, 1)
                    elif name == "EXP3" and slot.has("SUM"):
                        tok_exps(act, slot)
                    elif name == "HALF" and slot.middle:
                        wait(act, pv_done, slot, lambda t: PV_GROUPS * (t - 1) + 2 * n + 2)
                        wait(act, attn_ready, slot, lambda t: 2 * (t - 1) + n)
                        act.activation(first_v[:, :], pv[:, 0], ACT.Copy, scale=low16)
                        act.activation(second_sum[:, :], pv[:, 1], ACT.Copy, scale=low16).then_inc(parts_ready, 1)
                    elif name == "LN1" and slot.next_front:
                        ln_apply(act, slot, 0)
                    elif name == "CHI" and slot.back:
                        split_state_hi(slot)
                    elif name == "E" and slot.middle:
                        if n % 3 == 0:
                            wait(act, pv_done, slot, lambda t: PV_GROUPS * (t - 1) + n // 3 - 1)
                        wait(act, s2_full, slot, lambda t: S2_BANKS * (t - 1) + n + 1)
                        act.activation(probs[:, n % PROB_RING, :], s2[:, n % 2, :], ACT.Exp, scale=SCALE)\
                           .then_inc(probs_ready, 1)

            all_slots(act, slot_act)

            with act.Fori(0, IMAGES) as k:
                at = bass.ds((k + RING) % IMAGES * IMG, IMG)
                act.wait_ge(pre_ready, k + 1)
                act.activation(xo[:, at], xo[:, at], ACT.Tanh).then_inc(tanh_ready, 1)

        @block.vector
        def _(dve):
            dve.memset(same_image[:, :], 0.0)
            dve.memset(eps[:, :], EPS)
            dve.memset(spare[:, :], 0.0).then_inc(dve_set, 1)
            dve.wait_ge(dve_set, 1)
            for i in range(2):
                dve.memset(same_image[64 * i:64 * (i + 1), 64 * i:64 * (i + 1)], 1.0).then_inc(consts_set, 1)
            dve.memset(neg_half[:, :], -0.5).then_inc(consts_set, 1)
            dve.memset(dots[:, 0:3], 0.0)
            dve.memset(logit_b[:, 1:2], 0.0)
            dve.memset(logit_b[:, 2:3], MASKED)
            for g, lv in enumerate((3, 3, 2, 1)):
                dve.memset(logit_s[:, 3 * g:3 * g + 3], 0.5 ** lv)
                dve.memset(band_s[:, 3 * g:3 * g + 3], 0.25 ** lv)
            dve.memset(c2[:, :, :], 0.0).then_inc(c_half, 1)
            dve.wait_ge(tok_in, 16)
            dve.wait_ge(consts_set, 7)
            tok_forward(dve, FIRST_PAIR)
            dve.wait_ge(tokw_in, 16)
            dve.wait_ge(c_half, 1)
            for piece in range(len(DOT_PIECES)):
                tok_dots(dve, FIRST_PAIR, piece)
            dve.wait_ge(small_in, 80)
            tok_logits(dve, FIRST_PAIR)
            for m in range(KT):
                dve.tensor_scalar(c2[:, m, :], c2[:, m, :], half_col[:, 3, m:m + 1], 2.0, ALU.add, ALU.mult)
            dve.tensor_scalar(gate_b[:, 0:2, :], half_col[:, 0:2, :], 0.5, None, ALU.mult)
            dve.tensor_copy(gate_b[:, 2, :], half_col[:, 2, :]).then_inc(c_ready, 1)
            tok_softmax(dve, FIRST_PAIR)
            small_wait(dve, FIRST_PAIR, SMALL)
            tok_backward(dve, FIRST_PAIR)
            dve.wait_ge(hidden_in[0], HIDDEN_DMAS)
            ln_stats(dve, BEFORE_FIRST, 0)
            ln_shift(dve, BEFORE_FIRST, 0)

            def split_state_lo(slot):
                wait(dve, c_hi_ready, slot, lambda t: t)
                dve.scalar_tensor_tensor(out=c_split[1][:, :, :], in0=c2[:, :, :], scalar=0.5, in1=c_split[0][:, :, :],
                                         op0=ALU.mult, op1=ALU.subtract).then_inc(c_lo_ready, 1)

            split_state_lo(START)

            def slot_dve(now):
                if now.t == 1:
                    dve.wait_ge(rest_in, 16)
                    dve.tensor_scalar(w_all[:, UX], w_all[:, UX], 0.5, None, ALU.mult).then_inc(u_scaled, 1)
                for name, n, slot in now.steps(DVE_ORDER):
                    if name == "NEG" and slot.middle:
                        wait(dve, s1_emptied, slot, lambda t: S1_BANKS * t)
                        dve.tensor_scalar(neg_max_parts[:, :, 0, :], row_max[:, :, :], -1.0, None, ALU.mult)\
                           .then_inc(max_part1, 1)
                        wait(dve, max_part1, slot, lambda t: t)
                        dve.scalar_tensor_tensor(out=neg_max_parts[:, :, 1, :], in0=row_max[:, :, :], scalar=-1.0,
                                                 in1=neg_max_parts[:, :, 0, :], op0=ALU.mult, op1=ALU.subtract)\
                           .then_inc(max_parts_ready, 1)
                    elif name == "WO" and slot.back:
                        full(dve, slot, "WO")
                        h = residual(slot, 2)
                        dve.tensor_tensor(h, h, bank("WO"), ALU.add).then_inc(stage_emptied[JOB_BANK["WO"]], 1)
                    elif name == "STATS2" and slot.back:
                        emptied(dve, slot, "WO")
                        ln_stats(dve, slot, 1)
                    elif name == "Q" and slot.front:
                        wait(dve, q1_ready, slot, lambda t: t + 1)
                        dve.tensor_tensor(q_rest[:, :], bank("Q"), q_parts[:, 0].rearrange("p m t -> p (m t)"),
                                          ALU.subtract).then_inc(stage_emptied[JOB_BANK["Q"]], 1)
                    elif name == "K" and slot.front:
                        wait(dve, k1_ready, slot, lambda t: t + 1)
                        dve.tensor_tensor(k_rest[:, :], bank("K"), k_parts[:, 0].rearrange("p m t -> p (m t)"),
                                          ALU.subtract).then_inc(stage_emptied[JOB_BANK["K"]], 1)
                    elif name == "Q3" and slot.front:
                        wait(dve, q2_ready, slot, lambda t: t + 1)
                        dve.tensor_tensor(q_parts[:, 2].rearrange("p m t -> p (m t)"), q_rest[:, :],
                                          q_parts[:, 1].rearrange("p m t -> p (m t)"), ALU.subtract)\
                           .then_inc(q3_ready, 1)
                    elif name == "K3" and slot.front:
                        wait(dve, k2_ready, slot, lambda t: t + 1)
                        dve.tensor_tensor(k_parts[:, 2].rearrange("p m t -> p (m t)"), k_rest[:, :],
                                          k_parts[:, 1].rearrange("p m t -> p (m t)"), ALU.subtract)\
                           .then_inc(k3_ready, 1)
                    elif name == "LOGITS" and slot.has("SUM"):
                        tok_logits(dve, slot)
                    elif name == "C" and slot.back:
                        f, i, g = (gate[:, a].rearrange("p m t -> p (m t)") for a in range(3))
                        c = c2[:, :, :].rearrange("p m t -> p (m t)")
                        if n == 0:
                            emptied(dve, slot, "F")
                            dve.scalar_tensor_tensor(out=f, in0=f, scalar=1.0, in1=c, op0=ALU.add, op1=ALU.mult)
                        else:
                            emptied(dve, slot, "I")
                            emptied(dve, slot, "G")
                            dve.scalar_tensor_tensor(out=i, in0=i, scalar=1.0, in1=g, op0=ALU.add, op1=ALU.mult)\
                               .then_inc(c_half, 1)
                            wait(dve, c_half, slot, lambda t: t)
                            dve.scalar_tensor_tensor(out=c, in0=f, scalar=0.5, in1=i, op0=ALU.mult, op1=ALU.add)\
                               .then_inc(c_ready, 1)
                    elif name == "CLO" and slot.back:
                        split_state_lo(slot)
                    elif name in ("XT1", "XT2") and slot.has(name):
                        which = int(name[2]) - 1
                        wait(dve, xt_hi_ready[which], slot, lambda t: t + 1 - 2 * which)
                        dve.tensor_tensor(xt[1][:, :, :], bank(name).rearrange("p (k t) -> p k t", k=KT), xt[0][:, :, :],
                                          ALU.subtract).then_inc(stage_emptied[JOB_BANK[name]], 1)
                    elif name == "DOTS" and slot.has("SUM"):
                        tok_dots(dve, slot, n)
                    elif name == "SHIFT2" and slot.back:
                        ln_shift(dve, slot, 1)
                    elif name == "SOFTMAX" and slot.has("SUM"):
                        tok_softmax(dve, slot)
                    elif name == "STATS1" and slot.next_front:
                        wait(dve, hidden_in[1 - slot.par], slot, lambda t: HIDDEN_DMAS * ((t + 1) // 2 + 1))
                        ln_stats(dve, slot, 0)
                    elif name == "SHIFT1" and slot.next_front:
                        ln_shift(dve, slot, 0)
                    elif name == "M" and slot.front:
                        wait(dve, s1_full, slot, lambda t: S1_BANKS * t + n + 1)
                        if n >= 4:
                            dve.tensor_reduce(row_max[:, 1, 2 * n - 8:2 * n - 6],
                                              s1[:, n % S1_RING, :].rearrange("p (h k) -> p h k", h=2), AX_X, ALU.max)\
                               .then_inc(s1_emptied, 1)
                        else:
                            dve.memset(max_spare[:, n:n + 1], 0.0)
                            for m in range(4):
                                at = s1[:, n % S1_RING, m * P:(m + 1) * P]
                                last = dve.tensor_tensor_reduce(at, at, mask_qk[:, :], 1.0, LOWEST, ALU.add, ALU.max,
                                                                row_max[:, 0, 4 * n + m:4 * n + m + 1])
                            last.then_inc(s1_emptied, 1)
                    elif name == "HALF" and slot.middle:
                        here = lambda t: 2 * (t - 1) + n + 1
                        wait(dve, parts_ready, slot, here)
                        dve.scalar_tensor_tensor(out=row_sum[:, :], in0=pv[:, 0], scalar=high16,
                                                 in1=second_sum[:, :], op0=ALU.mult, op1=ALU.add).then_inc(sum_ready, 1)
                        dve.scalar_tensor_tensor(out=attn_t[:, n], in0=pv[:, 1], scalar=high16,
                                                 in1=first_v[:, :], op0=ALU.mult, op1=ALU.add).then_inc(pair_ready, 1)
                        wait(dve, sum_ready, slot, here)
                        dve.memset(spare[:, :], 0.0)
                        dve.stream_shuffle(row_inv[:, :], row_sum[:, :], [*range(DH, 2 * DH), *range(DH)])\
                           .then_inc(turned_ready, 1)
                        wait(dve, turned_ready, slot, here)
                        dve.reciprocal(row_inv[:, :], row_inv[:, :]).then_inc(inv_ready, 1)
                        wait(dve, inv_ready, slot, here)
                        dve.tensor_tensor(attn_t[:, n], attn_t[:, n], row_inv[:, :], ALU.mult)\
                           .then_inc(attn_ready, 1)

            all_slots(dve, slot_dve)

            dve.wait_ge(stage_full[1], job_number(1) + 1)
            dve.tensor_tensor(cu[:, :, :], stage[:, 1, :].rearrange("p (i c) -> p i c", i=TILES),
                              bo_row[:, :].unsqueeze(1).to_broadcast([P, TILES, D]), ALU.add).then_inc(cu_ready, 1)
            dve.wait_ge(cu_ready, 1)
            dve.wait_ge(stage_emptied[1], job_number(1))
            flat_cu = cu[:, :, :].rearrange("p i c -> p (i c)")

            def pre(at):
                dve.tensor_tensor(xo[:, at], xo[:, at], flat_cu, ALU.add).then_inc(pre_ready, 1)

            def place_of(j):
                return bass.ds((j + RING) % IMAGES * IMG, IMG)

            def finish_odd(k, kept, first):
                at = place_of(2 * k + 1)
                dve.wait_ge(tanh_ready, 2 * k + 2)
                dve.tensor_tensor(xo[:, at], xo[:, at], kept[:, bass.ds((2 * k + 1 - first) * IMG, IMG)], ALU.add)\
                   .then_inc(out_odd, 1)

            pre(place_of(0))
            pre(place_of(1))
            with dve.Fori(0, RING // 2) as k:
                pre(place_of(2 * k + 2))
                pre(place_of(2 * k + 3))
                finish_odd(k, hidden, 0)
            for par in range(2):
                dve.wait_ge(reloaded[par], 16)
            with dve.Fori(RING // 2, IMAGES // 2 - 1) as k:
                pre(place_of(2 * k + 2))
                pre(place_of(2 * k + 3))
                finish_odd(k, early, RING)
            finish_odd(IMAGES // 2 - 1, early, RING)

        @block.tensor
        def _(pe):
            pe.wait_ge(consts_set, 7)
            pe.wait_ge(dots_done, DOTS)
            tok_sum_matmul(pe)

            def begin(slot, job):
                wait(pe, stage_emptied[JOB_BANK[job]], slot, lambda t: jobs_before(t, job))

            def transposes(job):
                out4 = bank(job).rearrange("p (k t) -> p k t", k=KT)
                for i in range(TILES):
                    for k in range(KT):
                        last = pe.transpose(out4[:, k, i * P:(i + 1) * P], xn[:, i, k * P:(k + 1) * P], ident[:, :])
                last.then_inc(stage_full[JOB_BANK[job]], 1)

            def product(dst, terms):
                for n, (lhs, rhs) in enumerate(terms):
                    last = pe.matmul(dst, lhs, rhs, start=(n == 0), stop=(n == len(terms) - 1))
                return last

            def split_terms(a, b, cols_a, cols_b):
                return [(a[i][:, k, cols_a], b[j][:, k, cols_b]) for k in range(KT) for i, j in ((0, 0), (1, 0), (0, 1))]

            def split_weight(w):
                return w_hi[:, w], w_lo[:, w]

            EVERY = slice(0, S)

            def by_feature(job, w, u=None):
                for m in range(2):
                    cols = slice(m * P, (m + 1) * P)
                    terms = split_terms(split_weight(w), xt, cols, EVERY)
                    if u is not None:
                        terms += split_terms(split_weight(u), c_split, cols, EVERY)
                    last = product(bank(job)[:, m * S:(m + 1) * S], terms)
                last.then_inc(stage_full[JOB_BANK[job]], 1)

            def by_token(b, terms):
                for i in range(TILES):
                    last = product(stage[:, b, i * D:(i + 1) * D], terms(slice(i * P, (i + 1) * P)))
                last.then_inc(stage_full[b], 1)

            def whole_terms(xt, w):
                return lambda toks: [(xt[:, k, toks], w_all[:, w, k, :]) for k in range(KT)]

            def job_matmuls(slot, job):
                if job == "WO":
                    begin(slot, job)
                    wait(pe, attn_ready, slot, lambda t: 2 * (t - 1))
                    if slot.k is None and slot.t == 2:
                        pe.wait_ge(rest_in, 16)
                        pe.wait_ge(u_scaled, 1)
                    by_token(JOB_BANK[job], whole_terms(attn_t, WO))
                elif job == "XT1":
                    begin(slot, job)
                    wait(pe, xn_ready[0], slot, lambda t: t + 1)
                    transposes(job)
                elif job in "QK":
                    begin(slot, job)
                    if job == "Q":
                        emptied(pe, slot, "XT1")
                    if slot.k is None and slot.t == 0:
                        pe.wait_ge(w_lo_ready, len(SPLIT))
                    by_feature(job, WQ if job == "Q" else WK)
                elif job == "V":
                    begin(slot, job)
                    by_token(JOB_BANK[job], lambda toks: split_terms(xt, split_weight(WV), toks, EVERY))
                elif job == "SUM":
                    begin(slot, job)
                    wait(pe, dots_done, slot, lambda t: DOTS * (t // 2 + 2))
                    tok_sum_matmul(pe)
                elif job == "XT2":
                    begin(slot, job)
                    wait(pe, xn_ready[1], slot, lambda t: t - 1)
                    transposes(job)
                elif job in "FIG":
                    begin(slot, job)
                    if job == "F":
                        emptied(pe, slot, "XT2")
                        wait(pe, c_lo_ready, slot, lambda t: t - 1)
                    g = "FIG".index(job)
                    by_feature(job, WF + g, UF + g)
                elif job == "X":
                    begin(slot, job)
                    by_token(JOB_BANK[job], lambda toks: split_terms(xt, split_weight(WX), toks, EVERY))
                elif job == "MT":
                    wait(pe, probs_ready, slot, lambda t: S2_BANKS * (t - 1))
                    wait(pe, max_parts_ready, slot, lambda t: t)
                    for i in range(TILES):
                        last = pe.transpose(mt_rows[:, i * P:(i + 1) * P],
                                            neg_max_parts[:, i].rearrange("p a h -> p (a h)"), ident_b[:, :])
                    last.then_inc(mt_full, 1)

            def max_scores(slot, n):
                if n == 0:
                    wait(pe, q_stacked, slot, lambda t: 96 * (t + 1))
                    wait(pe, k_stacked, slot, lambda t: 96 * (t + 1))
                wait(pe, s1_emptied, slot, lambda t: S1_BANKS * t + n + 1 - S1_RING)
                dst = s1[:, n % S1_RING, :]
                heads, keys, i = (range(4 * n, 4 * n + 4), P, 0) if n < 4 else (range(2 * (n - 4), 2 * (n - 4) + 2), S, 1)
                by_head = dst.rearrange("p (h k) -> p h k", k=keys)
                if i == 1:
                    pe.matmul(by_head[:, :, P:S], ident_b[:, :], mask_qk[:, :].unsqueeze(1).to_broadcast([P, 2, P]),
                              start=True, stop=False, skip_group_check=True)
                for m, h in enumerate(heads):
                    last = pe.matmul(by_head[:, m, :], q_stack[0:QK_ROWS, slot.par, h, i * P:(i + 1) * P],
                                     k_stack[0:QK_ROWS, slot.par, h, 0:keys], start=(i == 0), stop=True,
                                     skip_group_check=True)
                last.then_inc(s1_full, 1)

            def place(h):
                return 2 * (h % (HEADS // 2)) + h // (HEADS // 2)

            def group_heads(g):
                return [8 * (g // 2) + 2 * j + g % 2 for j in range(4)]

            def exp_scores(slot, n):
                g, part = divmod(n, 3)
                par = 1 - slot.par
                if n == 0:
                    wait(pe, max_stacked, slot, lambda t: 16 * t)
                    if slot.k is None:
                        pe.wait_ge(pads_set, 4)
                wait(pe, probs_ready, slot, lambda t: S2_BANKS * (t - 1) + n - 1)
                heads = group_heads(g)[2 * part:2 * part + 2] if part < 2 else group_heads(g)
                i, queries = (0, S) if part < 2 else (1, P)
                by_head = s2[:, n % 2, :].rearrange("p (h q) -> p h q", q=queries)
                pe.matmul(by_head[:, :, 0:P], ident_b[:, :], mask_kq[:, :].unsqueeze(1).to_broadcast([P, len(heads), P]),
                          start=True, stop=False, skip_group_check=True)
                for m, h in enumerate(heads):
                    last = pe.matmul(by_head[:, m, :], k_stack[0:S2_ROWS, par, place(h), i * P:(i + 1) * P],
                                     q_stack[0:S2_ROWS, par, place(h), S - queries:S], start=False, stop=True,
                                     skip_group_check=True)
                last.then_inc(s2_full, 1)

            def times_v(slot, g):
                half, which = divmod(g, 2)
                par = 1 - slot.par
                wait(pe, probs_ready, slot, lambda t: S2_BANKS * (t - 1) + 3 * (g + 1))
                if which == 0:
                    wait(pe, pair_ready, slot, lambda t: 2 * (t - 1) + half)
                for i, queries in ((0, S), (1, P)):
                    for j, h in enumerate(group_heads(g)):
                        b = (3 * g + (j // 2 if i == 0 else 2)) % PROB_RING
                        m = j % 2 if i == 0 else j
                        lhs = v_pad[:, par, i, h // 2, 2 * which:2 * which + 2, :].rearrange("p a r -> p (a r)")
                        last = pe.matmul(pv[32 * j:32 * (j + 1), which, S - queries:S], lhs,
                                         probs[:, b, m * queries:(m + 1) * queries],
                                         start=(which == 0 and i == 0), stop=(which == 1 and i == 1),
                                         skip_group_check=True)
                last.then_inc(pv_done, 1)

            def slot_pe(now):
                for name, n, slot in now.steps(PE_ORDER):
                    if name == "S1":
                        if slot.front:
                            max_scores(slot, n)
                    elif name == "S2":
                        if slot.middle:
                            exp_scores(slot, n)
                    elif name == "PV":
                        if slot.middle:
                            times_v(slot, n)
                    elif slot.has(name):
                        job_matmuls(slot, name)

            all_slots(pe, slot_pe)

            pe.wait_ge(stage_emptied[1], job_number(1))
            pe.wait_ge(c_ready, IMAGES + 1)
            by_token(1, whole_terms(c2, UX))


def _lay_out(inputs):
    a = {k: np.asarray(v) for k, v in inputs.items()}

    def tiles(w):
        return w.reshape(KT, P, D).transpose(1, 0, 2)

    def by_row_of_head(w):
        return w.reshape(D, 2, HEADS // 2, DH).transpose(0, 1, 3, 2).reshape(D, D)

    mats = [by_row_of_head(a["L0_attn_Wq"].T), by_row_of_head(a["L0_attn_Wk"].T), a["L0_attn_Wv"].T]
    mats += [a["L0_ffn_" + n].T for n in ("wf", "wi", "wc", "wo", "uf", "ui", "uc")]
    mats += [a["L0_attn_Wo"].T, a["L0_ffn_uo"].T]
    weights = np.stack([tiles(m) for m in mats], axis=1)

    vhd = [1, 0, 2]
    parts = []
    for lv, name in ((1, "Wd3"), (2, "Wd2"), (3, "Wd1")):
        rows, cols = (S >> lv) // 32, (D >> lv) // 2
        w = a["L0_tok_" + name].reshape(3, 32, rows, 2, cols, 3)[vhd][..., vhd]
        parts.append(w.transpose(1, 3, 5, 0, 2, 4).reshape(64, 9 * BAND[lv - 1]))
    parts.append(a["L0_tok_Wa"].reshape(32, 1, 2, 16).transpose(0, 2, 1, 3).reshape(64, BAND[2]))
    tok_w = np.concatenate(parts, axis=1)
    tok_w = np.concatenate([tok_w, tok_w], axis=0)
    tok_b = np.concatenate([a["L0_tok_ba"]] + [a["L0_tok_" + n][vhd] for n in ("bd1", "bd2", "bd3")])

    x = a["x"].reshape(PAIRS, 2, S // BR, BR, 2, BC).transpose(0, 1, 2, 4, 3, 5).reshape(PAIRS, P, XW)
    col_b = np.stack([a["L0_ffn_" + n].reshape(KT, P).T for n in ("bf", "bi", "bc", "in_c")], axis=1)
    high = (np.arange(P) // DH % 2).astype(np.float32)
    halves = np.stack([1 - high, high], axis=1)
    arrays = {"x_in": x, "weights_in": weights, "tok_w_in": tok_w, "tok_b_in": tok_b, "col_b_in": col_b,
              "bo_in": a["L0_ffn_bo"], "halves_in": halves}
    return {k: np.ascontiguousarray(v) for k, v in arrays.items()}


def kernel(**inputs):
    import concourse.bacc as bacc
    from concourse.bass_utils import run_bass_kernel_spmd

    nc = bacc.Bacc("TRN2", target_bir_lowering=False, num_devices=1)
    arrays = _lay_out(inputs)
    args = [nc.dram_tensor(k, v.shape, mybir.dt.from_np(v.dtype), kind="ExternalInput").ap() for k, v in arrays.items()]
    out = nc.dram_tensor("out", (IMAGES, S, D), F32, kind="ExternalOutput").ap()
    scratch = nc.dram_tensor("scratch", (PAIRS, P, XW), F32, kind="Internal").ap()
    spill = nc.dram_tensor("spill", (IMAGES, P, IMG), F32, kind="Internal").ap()
    build(nc, *args, out, scratch, spill)
    result = run_bass_kernel_spmd(nc, [arrays], core_ids=[0])
    return result.results[0]["out"]
```
